# Optimizing a Trainium2 kernel written in Bass

```python
import numpy as np
import jax
import jax.numpy as jnp

def _softmax(x, axis=-1):
    return jax.nn.softmax(x, axis=axis)

def _gelu(x):
    return jax.nn.gelu(x, approximate=True)

def _silu(x):
    return jax.nn.silu(x)

def _sigmoid(x):
    return jax.nn.sigmoid(x)

def _layernorm(x, axis=-1, eps=1e-05):
    m = jnp.mean(x, axis=axis, keepdims=True)
    v = jnp.var(x, axis=axis, keepdims=True)
    return (x - m) / jnp.sqrt(v + eps)

def _scatter_add(tgt, idx, src, axis=0):
    return tgt.at[idx].add(src)

def _segment_sum(src, seg, n):
    return jax.ops.segment_sum(src, seg, n)
kernel_name = 'mk_gnn_ffn_d1_gnn_r8_cc99c3'

def setup_inputs(seed: int=0):
    np.random.seed(seed)
    _w = jnp.asarray

    def _rec_inputs():
        import jax
        import jax.numpy as jnp
        _gk = jax.random.key(seed)
        x = 0.0001963 + 1 * jax.random.normal(jax.random.fold_in(_gk, 1), (12500, 256), jnp.float32)
        src = jax.random.randint(jax.random.fold_in(_gk, 2), (200000,), 0, 12500, jnp.int32)
        dst = jnp.minimum((12500 * jax.random.uniform(jax.random.fold_in(_gk, 3), (200000,)) ** 2.0).astype(jnp.int32), 99999)
        _o = jnp.argsort(dst, stable=True)
        src = src[_o]
        dst = dst[_o]
        return (x, src, dst)
    x, src, dst = _rec_inputs()

    def _L0_gnn_setup():
        import jax, jax.numpy as jnp
        import numpy as np
        N_NODES = 12500
        N_EDGES = 40000
        DIM = 256

        def _graph_conv(src, dst, h, W, b):
            ones = jnp.ones((src.shape[0],), dtype=h.dtype)
            out_deg = jnp.clip(jax.ops.segment_sum(ones, src, num_segments=N_NODES), 1.0)
            in_deg = jnp.clip(jax.ops.segment_sum(ones, dst, num_segments=N_NODES), 1.0)
            h = h * (out_deg ** (-0.5))[:, None]
            agg = jax.ops.segment_sum(h[src], dst, num_segments=N_NODES)
            agg = agg * (in_deg ** (-0.5))[:, None]
            return agg @ W + b
        key = jax.random.key(seed)
        ks = jax.random.split(key, 7)
        src = jax.random.randint(ks[0], (N_EDGES,), 0, N_NODES, dtype=jnp.int32)
        dst = jax.random.randint(ks[1], (N_EDGES,), 0, N_NODES, dtype=jnp.int32)
        node_feature = jax.random.normal(ks[2], (N_NODES, DIM), dtype=jnp.float32)
        s = 1.0 / np.sqrt(DIM)
        W1 = jax.random.normal(ks[3], (DIM, DIM), dtype=jnp.float32) * s
        b1 = jnp.zeros((DIM,), dtype=jnp.float32)
        W2 = jax.random.normal(ks[4], (DIM, DIM), dtype=jnp.float32) * s
        b2 = jnp.zeros((DIM,), dtype=jnp.float32)
        return {'src': src, 'dst': dst, 'node_feature': node_feature, 'W1': W1, 'b1': b1, 'W2': W2, 'b2': b2}
    _L0_gnn_all = _L0_gnn_setup()
    _L0_gnn_in = {k: v for k, v in _L0_gnn_all.items() if k in ('W1', 'b1', 'W2', 'b2')}
    del _L0_gnn_all

    def _L0_ffn_setup():
        import jax, jax.numpy as jnp
        import numpy as np
        E, D, H, TOP_K = (6, 256, 256, 2)
        ROUTER_H = D // 2
        key = jax.random.key(seed)
        ks = jax.random.split(key, 12)
        s = 1.0 / np.sqrt(D)
        sh = 1.0 / np.sqrt(H)
        sr = 1.0 / np.sqrt(ROUTER_H)
        return {'features': jax.random.normal(ks[0], (8, 512, D), dtype=jnp.float32), 'router_w1': jax.random.uniform(ks[1], (D, ROUTER_H), jnp.float32, -s, s), 'router_b1': jnp.zeros((ROUTER_H,), jnp.float32), 'router_w2': jax.random.uniform(ks[2], (ROUTER_H, E), jnp.float32, -sr, sr), 'router_b2': jnp.zeros((E,), jnp.float32), 'expert_w1': jax.random.uniform(ks[3], (E, D, H), jnp.float32, -s, s), 'expert_b1': jnp.zeros((E, H), jnp.float32), 'expert_w2': jax.random.uniform(ks[4], (E, H, H), jnp.float32, -sh, sh), 'expert_b2': jnp.zeros((E, H), jnp.float32), 'expert_w3': jax.random.uniform(ks[5], (E, H, D), jnp.float32, -sh, sh), 'expert_b3': jnp.zeros((E, D), jnp.float32)}
    _L0_ffn_all = _L0_ffn_setup()
    _L0_ffn_in = {k: v for k, v in _L0_ffn_all.items() if k in ('router_w1', 'router_b1', 'router_w2', 'router_b2', 'expert_w1', 'expert_b1', 'expert_w2', 'expert_b2', 'expert_w3', 'expert_b3')}
    del _L0_ffn_all
    return {'x': x, 'src': src, 'dst': dst, 'L0_gnn_W1': _L0_gnn_in['W1'], 'L0_gnn_b1': _L0_gnn_in['b1'], 'L0_gnn_W2': _L0_gnn_in['W2'], 'L0_gnn_b2': _L0_gnn_in['b2'], 'L0_ffn_router_w1': _L0_ffn_in['router_w1'], 'L0_ffn_router_b1': _L0_ffn_in['router_b1'], 'L0_ffn_router_w2': _L0_ffn_in['router_w2'], 'L0_ffn_router_b2': _L0_ffn_in['router_b2'], 'L0_ffn_expert_w1': _L0_ffn_in['expert_w1'], 'L0_ffn_expert_b1': _L0_ffn_in['expert_b1'], 'L0_ffn_expert_w2': _L0_ffn_in['expert_w2'], 'L0_ffn_expert_b2': _L0_ffn_in['expert_b2'], 'L0_ffn_expert_w3': _L0_ffn_in['expert_w3'], 'L0_ffn_expert_b3': _L0_ffn_in['expert_b3']}

def reference(x, src, dst, L0_gnn_W1, L0_gnn_b1, L0_gnn_W2, L0_gnn_b2, L0_ffn_router_w1, L0_ffn_router_b1, L0_ffn_router_w2, L0_ffn_router_b2, L0_ffn_expert_w1, L0_ffn_expert_b1, L0_ffn_expert_w2, L0_ffn_expert_b2, L0_ffn_expert_w3, L0_ffn_expert_b3):
    import jax
    import jax.numpy as jnp

    def _L0_gnn_ref(src, dst, node_feature, W1, b1, W2, b2):
        import jax, jax.numpy as jnp
        import numpy as np
        N_NODES = 12500
        N_EDGES = 40000
        DIM = 256

        def _graph_conv(src, dst, h, W, b):
            ones = jnp.ones((src.shape[0],), dtype=h.dtype)
            out_deg = jnp.clip(jax.ops.segment_sum(ones, src, num_segments=N_NODES), 1.0)
            in_deg = jnp.clip(jax.ops.segment_sum(ones, dst, num_segments=N_NODES), 1.0)
            h = h * (out_deg ** (-0.5))[:, None]
            agg = jax.ops.segment_sum(h[src], dst, num_segments=N_NODES)
            agg = agg * (in_deg ** (-0.5))[:, None]
            return agg @ W + b
        h = _graph_conv(src, dst, node_feature, W1, b1)
        h = _graph_conv(src, dst, jax.nn.relu(h), W2, b2)
        return jax.nn.relu(h)

    def _L0_ffn_ref(features, router_w1, router_b1, router_w2, router_b2, expert_w1, expert_b1, expert_w2, expert_b2, expert_w3, expert_b3):
        import jax, jax.numpy as jnp
        import numpy as np
        E, D, H, TOP_K = (6, 256, 256, 2)
        ROUTER_H = D // 2
        rh = jax.nn.relu(features @ router_w1 + router_b1)
        expert_logits = jax.nn.softmax(rh @ router_w2 + router_b2, axis=-1)
        top_w, top_i = jax.lax.top_k(expert_logits, TOP_K)
        routing_weights = jax.nn.softmax(top_w, axis=-1)
        h1 = jax.nn.relu(jnp.einsum('bsd,edh->bseh', features, expert_w1) + expert_b1)
        h2 = jax.nn.relu(jnp.einsum('bseh,ehf->bsef', h1, expert_w2) + expert_b2)
        expert_out = jnp.einsum('bsef,efo->bseo', h2, expert_w3) + expert_b3
        sel = jnp.take_along_axis(expert_out, top_i[:, :, :, None], axis=2)
        combined = jnp.sum(sel * routing_weights[..., None], axis=2)
        return combined
    x = x + _L0_gnn_ref(src, dst, _layernorm(x, axis=-1), L0_gnn_W1, L0_gnn_b1, L0_gnn_W2, L0_gnn_b2)
    x = x + _L0_ffn_ref(_layernorm(x, axis=-1)[None], L0_ffn_router_w1, L0_ffn_router_b1, L0_ffn_router_w2, L0_ffn_router_b2, L0_ffn_expert_w1, L0_ffn_expert_b1, L0_ffn_expert_w2, L0_ffn_expert_b2, L0_ffn_expert_w3, L0_ffn_expert_b3)[0]
    return x

_drawn_inputs = setup_inputs


def setup_inputs(seed=0):
    import zlib

    import numpy as np

    out = dict(_drawn_inputs(seed))
    spreads = {'L0_gnn_b1': (0.0, 0.1),
     'L0_gnn_b2': (0.0, 0.1),
     'L0_ffn_router_b1': (0.0, 0.1),
     'L0_ffn_router_b2': (0.0, 0.1),
     'L0_ffn_expert_b1': (0.0, 0.684),
     'L0_ffn_expert_b2': (0.0, 0.29),
     'L0_ffn_expert_b3': (0.0, 0.1)}
    factors = {}
    for name, (base, spread) in spreads.items():
        noise = np.random.default_rng([zlib.crc32(name.encode()), seed]).standard_normal(out[name].shape)
        drawn = base * np.exp(spread * noise) if base else spread * noise
        out[name] = jnp.asarray(drawn.astype(out[name].dtype))
    for name, factor in factors.items():
        out[name] = (out[name] * factor).astype(out[name].dtype)
    return out
```

```python
from contextlib import ExitStack

import concourse.bass as bass
from concourse import mybir

P = 128
WIN = 64
TPG = 2
EPG = TPG * P
GPI = 8
TPI = GPI * TPG
TPB = 4
BPI = TPI // TPB
CHUNK = TPI // 2
AGG_SLOTS = 2
FAR = 1.0e6

F32 = mybir.dt.float32
BF16 = mybir.dt.bfloat16
I32 = mybir.dt.int32
U32 = mybir.dt.uint32
ALU = mybir.AluOpType
ACT = mybir.ActivationFunctionType
X = mybir.AxisListType.X


V_BAD = 12
V_LOC = 15
V_IDX = 16


class Steps:

    def __init__(self, sem, credit=0):
        self.sem, self.n, self.it, self.per, self.start = sem, credit, None, 0, 0

    def inc(self, ins):
        ins.then_inc(self.sem, 1)
        self.n += 1

    def enter(self, it, per):
        self.it, self.per, self.start = it, per, self.n

    def leave(self, trips):
        assert self.n - self.start == self.per, (self.n - self.start, self.per)
        self.n, self.it = self.start + self.per * trips, None

    def now(self, ahead=0):
        n = self.n + ahead
        return n if self.it is None else self.it * self.per + n


def gnn_experts(nc, t, out):
    N, D = t["x"].shape
    E = t["src"].shape[0]
    NE, _, H = t["L0_ffn_expert_w1"].shape
    RH = t["L0_ffn_router_w1"].shape[1]
    assert D == 2 * P and H == 2 * P and RH == P and NE <= 8
    KD = D // P
    NB = -(-N // P)
    LAST = N - (NB - 1) * P
    ITERS = -(-E // (EPG * GPI))
    NG = ITERS * GPI
    NT = NG * TPG
    FULLG, REST = E // EPG, E % EPG
    RB = -(-NG // P)
    RP = NG // RB
    assert NG % RB == 0 and RP <= P
    NW = -(-N // WIN)
    COLS = N + WIN
    assert COLS >= NB * P and COLS >= NW * WIN and NB % 2 == 0
    XC = 7 if NB % 7 == 0 else 2
    NXC = NB // XC

    h_tab = [nc.dram_tensor(f"table{n + 1}", (N, D), F32, kind="Internal").ap() for n in range(2)]
    base_dram = nc.dram_tensor("base_list", (NG,), I32, kind="Internal").ap()

    ctx = ExitStack()
    with ctx:
        ctx.enter_context(nc.allow_non_contiguous_dma(reason="small bias columns and group bases"))

        def sb(name, shape, dt=F32):
            return ctx.enter_context(nc.sbuf_tensor(name, shape, dt))

        def sem(name):
            return ctx.enter_context(nc.semaphore(name))

        big = sb("big", [P, max(NB * D, KD * COLS)])
        xbig = big[:, 0:NB * D].rearrange("p (b d) -> p b d", d=D)
        aggT = big[:, 0:KD * COLS].rearrange("p (k n) -> p k n", k=KD)
        WE = 3 * NE * KD * H
        late = sb("late", [P, max(WE, 4 * RB * EPG)])
        rows = late[:, 0:4 * RB * EPG].rearrange("p (a b e) -> p a b e", a=4, e=EPG)
        src_i, dst_i = rows[:, 0, :, :].bitcast(I32), rows[:, 1, :, :].bitcast(I32)
        src_f, dst_f = rows[:, 2, :, :], rows[:, 3, :, :]
        loc_f = rows[:, 1, :, :]
        we = late[:, 0:WE].rearrange("p (l e k h) -> p l e k h", l=3, e=NE, k=KD)
        idxT = sb("idxT", [P, NT], I32)
        locT = sb("locT", [P, NT])
        OH = TPB * (P + NB)
        work = sb("work", [P, max(2 * NT + OH, 13 * D)])
        hiT, loT = work[:, 0:NT], work[:, NT:2 * NT]
        onehots = work[:, 2 * NT:2 * NT + OH].bitcast(BF16).rearrange("p (b n) -> p b n", b=2)
        hlo = onehots[:, :, 0:TPB * P].rearrange("p b (t n) -> p b t n", t=TPB)
        hhi = onehots[:, :, TPB * P:].rearrange("p b (t n) -> p b t n", t=TPB)
        wrows = work[:, 0:13 * D].rearrange("p (a d) -> p a d", d=D)
        xr = wrows[:, 0:2, :]
        acc = wrows[:, 2:4, :]
        xnT = wrows[:, 4:6, :].rearrange("p b (k n) -> p b k n", k=KD)
        h1T = wrows[:, 6:8, :].rearrange("p b (k n) -> p b k n", k=KD)
        h2T = wrows[:, 8:10, :].rearrange("p b (k n) -> p b k n", k=KD)
        xn = wrows[:, 10, :]
        hb = wrows[:, 11:13, :]
        base_f = sb("base_f", [P, RB])
        base_i = sb("base_i", [P, RB], I32)
        base_l = sb("base_l", [1, NG], I32)
        bad = sb("bad", [P, 2])
        fast = sb("fast", [P, 1])
        fast_i = sb("fast_i", [P, 1], I32)
        iota_i = sb("iota_i", [P, P], I32)
        iota_p = sb("iota_p", [P, 1], I32)
        iota_pf = sb("iota_pf", [P, 1])
        iota = sb("iota", [P, P])
        iota_hi = sb("iota_hi", [P, NB])
        ident = sb("ident", [P, P])
        ones = sb("ones", [P, P])
        zero_b = sb("zero_b", [P, P], BF16)
        zeros = sb("zeros", [P, D])
        cw = sb("cw", [P, 2, KD, D])
        cb = sb("cb", [P, 2, D])
        rw1 = sb("rw1", [P, KD, RH])
        rb1 = sb("rb1", [P, 1])
        rw2 = sb("rw2", [P, NE])
        rb2 = sb("rb2", [P, NE])
        eb = sb("eb", [P, 2, NE, KD])
        eb3 = sb("eb3", [NE, D])
        out_s = sb("out_s", [P, NB])
        in_s = sb("in_s", [P, NB])
        deg = sb("deg", [P, NB])
        dtmp = sb("dtmp", [P, NB])
        mean = sb("mean", [P, NB])
        mdif = sb("mdif", [P, NB])
        rstd = sb("rstd", [P, NB])
        idx = [sb(f"idx{n}", [P, CHUNK], I32) for n in range(2)]
        gath = sb("gath", [P, GPI, TPG, D])
        stat = gath[:, :, :, :].rearrange("p g t d -> p (g t d)")[:, 0:NB * 6].rearrange("p (b s) -> p b s", s=6)
        oneh = sb("oneh", [P, BPI, TPB, WIN])
        locw = sb("locw", [P, TPG])
        stage = sb("stage", [P, 2, KD, P])
        tb = sb("tb", [P, 2, D])
        xin = sb("xin", [P, 2, D])
        st6 = sb("st6", [P, 6])
        mv = sb("mv", [P, 2])
        rs, rv, rt = (sb(n, [P, 1]) for n in ("rs", "rv", "rt"))
        rhT = sb("rhT", [P, P])
        lg = sb("lg", [P, NE])
        lmax = sb("lmax", [P, 1])
        pexp = sb("pexp", [P, NE])
        psumr = sb("psumr", [P, 1])
        prob = sb("prob", [P, 8])
        top = sb("top", [P, 8])
        topi = sb("topi", [P, 8], U32)
        topf = sb("topf", [P, 8])
        w12 = sb("w12", [P, 4])
        gate = sb("gate", [P, 2, NE])
        gt2 = sb("gt2", [P, NE])
        gateT = sb("gateT", [NE, P])

        def bank(name):
            return ctx.enter_context(nc.psum_tensor(name, [P, 512], F32))

        b_agg = [bank(f"b_agg{n}") for n in range(AGG_SLOTS)]
        b_front = [bank(f"b_front{n}") for n in range(2)]
        b_exp = [bank(f"b_exp{n}") for n in range(4)]
        p_agg = [b[:, 0:KD * WIN].rearrange("p (k w) -> p k w", k=KD) for b in b_agg]
        p_conv1 = [b[:, 0:D] for b in b_front]
        p_conv = b_front[0][:, 0:D]
        p_b3 = b_front[0][:, D:2 * D]
        p_rh = b_front[0][:, 0:P]
        p_gT = b_front[1][0:NE, 0:P]
        p_xnT = b_front[1][:, 0:D].rearrange("p (k n) -> p k n", k=KD)
        p_lg = b_front[1][:, D:D + NE]
        p_exp = [b[:, 0:D] for b in b_exp]
        p_deg = [b[:, 0:NB] for b in b_exp[0:2]]
        p_rows = [b[:, :].rearrange("p (a h n) -> p a h n", a=2, h=TPG) for b in b_front]
        p_bad = b_exp[2][0:RP, 0:1]

        filled = sem("filled")
        rows_in = sem("rows_in")
        consts_in = sem("consts_in")
        x_in = sem("x_in")
        vstep = sem("vstep")
        bad_sum = sem("bad_sum")
        flag_set = sem("flag_set")
        turned = sem("turned")
        unturned = sem("unturned")
        deg_oh = sem("deg_oh")
        deg_mm = sem("deg_mm")
        deg_end = sem("deg_end")
        bases_out = sem("bases_out")
        bases_in = sem("bases_in")
        normed = sem("normed")
        table_out = sem("table_out")
        agg_zero = sem("agg_zero")
        idx_set = [sem(f"idx_set{n}") for n in range(2)]
        rows_got = [sem(f"rows_got{n}") for n in range(GPI)]
        oh_set = sem("oh_set")
        agg_mm = sem("agg_mm")
        agg_add = sem("agg_add")
        gen_idx = sem("gen_idx")
        gen_rows = sem("gen_rows")
        gen_oh = sem("gen_oh")
        gen_mm = sem("gen_mm")
        gen_add = sem("gen_add")
        gen_loc = sem("gen_loc")
        passed = {n: sem(f"passed_{n}") for n in ("pool", "pe", "dve", "sp")}
        agg_done = sem("agg_done")
        staged = [sem(f"staged{n}") for n in range(2)]
        cleared = [sem(f"cleared{n}") for n in range(2)]
        conv_mm = [sem(f"conv_mm{n}") for n in range(2)]
        conv_ev = [sem(f"conv_ev{n}") for n in range(2)]
        hb_set = sem("hb_set")
        hb_out = [sem(f"hb_out{n}") for n in range(2)]
        hb_free = [sem(f"hb_free{n}") for n in range(2)]
        we_in = sem("we_in")
        xin_in = [sem(f"xin_in{n}") for n in range(2)]
        bstep = sem("bstep")
        xr_set = sem("xr_set")
        xn_set = sem("xn_set")
        xnT_mm = sem("xnT_mm")
        xnT_set = sem("xnT_set")
        rh_mm = sem("rh_mm")
        rh_set = sem("rh_set")
        lg_mm = sem("lg_mm")
        lmax_set = sem("lmax_set")
        pe_set = sem("pe_set")
        wd_set = sem("wd_set")
        wx_set = sem("wx_set")
        gate_set = sem("gate_set")
        gT_mm = sem("gT_mm")
        gT_set = sem("gT_set")
        b3_mm = sem("b3_mm")
        h1_mm = sem("h1_mm")
        h2_mm = sem("h2_mm")
        h3_mm = sem("h3_mm")
        h1_set = sem("h1_set")
        h2_set = sem("h2_set")
        acc_init = sem("acc_init")
        h3_ev = sem("h3_ev")
        acc_free = [sem(f"acc_free{n}") for n in range(2)]
        out_st = [sem(f"out_st{n}") for n in range(2)]

        block = ctx.enter_context(nc.Block())

        HB = NB // 2
        N_CONST = 2 * 2 + 4 + 2 * NE + 1
        N_ROWS = 2 * ((1 if FULLG // RP else 0) + (1 if FULLG % RP else 0) + (1 if REST else 0))
        N_FILL = 6
        DEG_ALL = ITERS * BPI

        def need(eng, semaphore, value):
            if not isinstance(value, int) or value > 0:
                eng.wait_ge(semaphore, value)

        def alone(eng, name):
            eng.sem_inc(passed[name], 1)

        def column(left, u):
            return left * (2 * P) + (1 - u) * P

        def expert_order():
            return [("l1", 0), ("l1", 1), ("gT", 0), ("conv", 0), ("l2", 0), ("l1", 2), ("l2", 1), ("b3", 0), ("l3", 0),
                    ("l1", 3), ("l2", 2), ("l3", 1), ("tr", 0), ("l1", 4), ("l2", 3), ("l3", 2), ("rh", 0),
                    ("l1", 5), ("l2", 4), ("l3", 3), ("lg", 0), ("l2", 5), ("l3", 4), ("l3", 5)]

        OUTPUTS = [x for x in expert_order() if x[0] in ("l1", "l2", "l3")]

        def exp_bank(what, e, v):
            return p_exp[(OUTPUTS.index((what, e)) + v * 3 * NE) % 4]

        def exp_before(what, e):
            at = OUTPUTS.index((what, e)) - 4
            return (*OUTPUTS[at], 1 if at < 0 else 0)

        def ahead(eng, q, n):
            return n - 1 - q if isinstance(q, int) else eng.snap(q * (-1) + (n - 1), min_val=0, max_val=n - 1)

        def bodies(eng, body):
            body(0, 0, True, False)
            with eng.Fori(0, HB - 1) as i:
                body(i, 1, True, True)
                body(i + 1, 0, True, True)
            body(HB - 1, 1, True, True)
            body(HB, 0, False, True)

        @block.sync
        def _(sp):
            sp.wait_ge(filled, 1)
            whole, part = FULLG // RP, FULLG % RP
            for name, rt in (("src", src_i), ("dst", dst_i)):
                if whole:
                    sp.dma_start(rt[0:RP, 0:whole, :], t[name][0:whole * RP * EPG].rearrange(
                        "(b p e) -> p b e", p=RP, e=EPG)).then_inc(rows_in, 16)
                if part:
                    sp.dma_start(rt[0:part, whole, :], t[name][whole * RP * EPG:FULLG * EPG].rearrange(
                        "(p e) -> p e", e=EPG)).then_inc(rows_in, 16)
                if REST:
                    sp.dma_start(rt[part:part + 1, whole, 0:REST], t[name][FULLG * EPG:E].rearrange(
                        "(p e) -> p e", p=1)).then_inc(rows_in, 16)
            for c in range(NXC):
                last = NB - 1 if c == NXC - 1 else (c + 1) * XC
                sp.dma_start(xbig[:, c * XC:last, :], t["x"][c * XC * P:last * P, :].rearrange(
                    "(b q) d -> q b d", q=P)).then_inc(x_in, 16)
            sp.dma_start(xbig[0:LAST, NB - 1, :], t["x"][(NB - 1) * P:N, :]).then_inc(x_in, 16)
            for n in range(2):
                sp.dma_start(cw[:, n, :, :], t[f"L0_gnn_W{n + 1}"].rearrange("(k p) d -> p k d", p=P)).then_inc(consts_in, 16)
                sp.dma_start(cb[:, n, :], t[f"L0_gnn_b{n + 1}"].partition_broadcast(P)).then_inc(consts_in, 16)
            sp.dma_start(rw1[:, :, :], t["L0_ffn_router_w1"].rearrange("(k p) h -> p k h", p=P)).then_inc(consts_in, 16)
            sp.dma_start(rb1[:, :], t["L0_ffn_router_b1"].rearrange("(p a) -> p a", a=1)).then_inc(consts_in, 16)
            sp.dma_start(rw2[:, :], t["L0_ffn_router_w2"]).then_inc(consts_in, 16)
            sp.dma_start(rb2[:, :], t["L0_ffn_router_b2"].partition_broadcast(P)).then_inc(consts_in, 16)
            for n in range(2):
                for e in range(NE):
                    sp.dma_start(eb[:, n, e, :], t[f"L0_ffn_expert_b{n + 1}"][e, :].rearrange(
                        "(k p) -> p k", p=P)).then_inc(consts_in, 16)
            sp.dma_start(eb3[:, :], t["L0_ffn_expert_b3"]).then_inc(consts_in, 16)
            sp.wait_ge(flag_set, 2)
            sp.dma_start(base_dram.rearrange("(b p) -> p b", p=RP), base_i[0:RP, :]).then_inc(bases_out, 16)
            sp.wait_ge(bases_out, 16)
            sp.dma_start(base_l[:, :], base_dram.rearrange("(a n) -> a n", a=1)).then_inc(bases_in, 16)
            for c in range(NXC):
                last = NB - 1 if c == NXC - 1 else (c + 1) * XC
                sp.wait_ge(normed, last)
                sp.dma_start(h_tab[0][c * XC * P:last * P, :].rearrange("(b q) d -> q b d", q=P),
                             xbig[:, c * XC:last, :]).then_inc(table_out, 16)
            sp.wait_ge(normed, NB)
            sp.dma_start(h_tab[0][(NB - 1) * P:N, :], xbig[0:LAST, NB - 1, :]).then_inc(table_out, 16)
            sp.wait_ge(turned, 2 * RB)
            for n in range(3):
                for e in range(NE):
                    sp.dma_start(we[:, n, e, :, :], t[f"L0_ffn_expert_w{n + 1}"][e, :, :].rearrange(
                        "(k p) h -> p k h", p=P)).then_inc(we_in, 16)
            for u in range(2):
                sp.sem_inc(hb_free[u], 1)
                sp.sem_inc(acc_free[u], 1)

            def store_hb(q, u, rows_n):
                row = column(ahead(sp, q, HB), u)
                sp.wait_ge(hb_set, 2 * q + (u + 2))
                alone(sp, "sp")
                sp.dma_start(h_tab[1][bass.ds(row, rows_n), :], hb[0:rows_n, u, :]).then_inc(hb_out[u], 16)
                sp.wait_ge(hb_out[u], q * 16 + 16)
                sp.sem_inc(hb_free[u], 1)

            store_hb(0, 0, LAST)
            store_hb(0, 1, P)
            with sp.Fori(1, HB) as i:
                for u in range(2):
                    store_hb(i, u, P)

            def load_x(q, u, rows_n):
                row = column(ahead(sp, q, HB), u)
                if not isinstance(q, int) or q > 0:
                    sp.wait_ge(xr_set, 2 * q + (u - 1))
                    alone(sp, "sp")
                sp.dma_start(xin[0:rows_n, u, :], t["x"][bass.ds(row, rows_n), :]).then_inc(xin_in[u], 16)

            def store_out(q, u, rows_n):
                row = column(ahead(sp, q, HB), u)
                if not isinstance(q, int) or q > 0:
                    sp.wait_ge(out_st[u], q * 16)
                    sp.sem_inc(acc_free[u], 1)
                sp.wait_ge(h3_ev, (2 * q + (u + 1)) * NE + 3)
                alone(sp, "sp")
                sp.dma_start(out[bass.ds(row, rows_n), :], acc[0:rows_n, u, :]).then_inc(out_st[u], 16)

            load_x(0, 0, LAST)
            load_x(0, 1, P)
            load_x(1, 0, P)
            store_out(0, 0, LAST)
            load_x(1, 1, P)
            store_out(0, 1, P)
            with sp.Fori(1, HB - 1) as i:
                for u in range(2):
                    load_x(i + 1, u, P)
                    store_out(i, u, P)
            store_out(HB - 1, 0, P)
            store_out(HB - 1, 1, P)
            for u in range(2):
                sp.wait_ge(out_st[u], 16 * HB)

        @block.gpsimd
        def _(pool):
            nc.gpsimd.memset(src_i[:, RB - 1, :], int(FAR))
            nc.gpsimd.memset(dst_i[:, RB - 1, :], int(FAR))
            nc.gpsimd.memset(xbig[:, NB - 1, :], 0.0)
            nc.gpsimd.memset(xin[:, 0, :], 0.0)
            pool.drain().then_inc(filled, 1)
            nc.gpsimd.iota(iota_i[:, :], pattern=[[1, P]], base=0, channel_multiplier=0).then_inc(filled, 1)
            nc.gpsimd.iota(iota_p[:, :], pattern=[[0, 1]], base=0, channel_multiplier=1).then_inc(filled, 1)
            nc.gpsimd.memset(ones[:, :], 1.0).then_inc(filled, 1)
            nc.gpsimd.memset(zero_b[:, :], 0.0).then_inc(filled, 1)
            nc.gpsimd.memset(zeros[:, :], 0.0).then_inc(filled, 1)
            pool.wait_ge(table_out, 16 * (NXC + 1))
            nc.gpsimd.memset(aggT[:, KD - 1, :], 0.0).then_inc(agg_zero, 1)
            pool.wait_ge(flag_set, 1)
            flag = nc.gpsimd.value_load(fast_i[0:1, 0:1], min_val=0, max_val=1)

            def gather_group(j, indices, k, tab, got):
                alone(pool, "pool")
                for h in range(TPG):
                    pool.indirect_dma_start(gath[:, j, h, :], None, tab, bass.IndirectOffsetOnAxis(
                        indices[:, k + h:k + h + 1], 0)).then_inc(got, 16)

            def gathers(layer):
                with pool.If(flag):
                    with pool.Fori(0, ITERS) as it:
                        for j in range(GPI):
                            c, k = divmod(j * TPG, CHUNK)
                            if k == 0:
                                pool.wait_ge(idx_set[c], it + (layer * ITERS + 1))
                            pool.wait_ge(agg_mm, it * GPI + (layer * ITERS * GPI + j + 1))
                            gather_group(j, idx[c], k, h_tab[layer], rows_got[j])
                with pool.Else():
                    with pool.Fori(0, NG) as g:
                        pool.wait_ge(gen_idx, g + (layer * NG + 1))
                        gather_group(0, idx[0], 0, h_tab[layer], gen_rows)

            gathers(0)
            with pool.Fori(0, HB) as i:
                left = ahead(pool, i, HB)
                for u in range(2):
                    pool.wait_ge(staged[u], i + 1)
                    nc.gpsimd.tensor_copy(aggT[:, :, bass.ds(column(left, u), P)],
                                          zeros[:, :].rearrange("p (k n) -> p k n", k=KD)).then_inc(cleared[u], 1)
            for u in range(2):
                pool.wait_ge(hb_out[u], 16 * HB)
            gathers(1)

        @block.scalar
        def _(act):
            act.sem_inc(h1_set, 2)
            act.sem_inc(h2_set, 2)
            act.wait_ge(flag_set, 1)
            flag = nc.scalar.value_load(fast_i[0:1, 0:1], min_val=0, max_val=1)

            def lay_indices(layer):
                with act.If(flag):
                    with act.Fori(0, ITERS) as it:
                        left = ahead(act, it, ITERS)
                        for c in range(2):
                            act.wait_ge(agg_mm, it * GPI + (layer * ITERS * GPI + (c + 1) * (GPI // 2)))
                            col = left * TPI + c * CHUNK
                            nc.scalar.copy(idx[c][:, :], idxT[:, bass.ds(col, CHUNK)]).then_inc(idx_set[c], 1)
                with act.Else():
                    with act.Fori(0, NG) as g:
                        act.wait_ge(gen_mm, g * NW + (layer * NG * NW + 1))
                        nc.scalar.copy(idx[0][:, 0:TPG], idxT[:, bass.ds(g * TPG, TPG)]).then_inc(gen_idx, 1)

            def stage_block(left, u, uses):
                act.wait_ge(conv_mm[u], uses + 1)
                nc.scalar.copy(stage[:, u, :, :], aggT[:, :, bass.ds(column(left, u), P)]).then_inc(staged[u], 1)

            act.wait_ge(vstep, V_IDX)
            lay_indices(0)
            act.wait_ge(agg_done, 1)
            with act.Fori(0, HB) as i:
                left = ahead(act, i, HB)
                for u in range(2):
                    stage_block(left, u, i)
            lay_indices(1)
            act.wait_ge(agg_done, 2)
            act.wait_ge(consts_in, 16 * N_CONST)

            def body(q, u, front, experts):
                m = 2 * q + u

                def rectify(ready, done, used, src, dst, layer, e):
                    src = src.rearrange("p (k n) -> p k n", k=KD)
                    k = (m - 1) * NE + e
                    act.wait_ge(ready, k + 3)
                    act.wait_ge(used, k + 1)
                    for c in range(KD):
                        ins = nc.scalar.activation(dst[:, e % 2, c, :], src[:, c, :], ACT.Relu,
                                                   bias=eb[:, layer, e, c:c + 1])
                    ins.then_inc(done, 1)

                if front:
                    stage_block(ahead(act, q, HB), u, q + HB)
                for what, e in expert_order():
                    if what == "l1" and experts:
                        rectify(h1_mm, h1_set, h2_mm, exp_bank("l1", e, 1 - u), h1T, 0, e)
                    if what == "l2" and experts:
                        rectify(h2_mm, h2_set, h3_mm, exp_bank("l2", e, 1 - u), h2T, 1, e)
                    if what == "gT" and experts:
                        act.wait_ge(gT_mm, m)
                        act.wait_ge(b3_mm, m)
                        nc.scalar.copy(gateT[:, :], p_gT).then_inc(gT_set, 1)
                    if what == "tr" and front:
                        act.wait_ge(xnT_mm, m + 1)
                        nc.scalar.copy(xnT[:, u, :, :], p_xnT).then_inc(xnT_set, 1)
                    if what == "rh" and front:
                        act.wait_ge(rh_mm, m + 1)
                        nc.scalar.activation(rhT[:, :], p_rh, ACT.Relu, bias=rb1[:, 0:1]).then_inc(rh_set, 1)
                    if what == "lg" and front:
                        act.wait_ge(lmax_set, m + 1)
                        nc.scalar.activation(pexp[:, :], lg[:, :], ACT.Exp, bias=lmax[:, 0:1],
                                             accum_out=psumr[:, 0:1]).then_inc(pe_set, 1)
                if front:
                    act.wait_ge(wd_set, m + 1)
                    nc.scalar.activation(w12[:, 1:2], w12[:, 0:1], ACT.Exp).then_inc(wx_set, 1)

            bodies(act, body)

        @block.tensor
        def _(pe):
            mm = nc.tensor.matmul
            pe.sem_inc(deg_mm, 2)
            pe.sem_inc(agg_mm, GPI)
            pe.sem_inc(gen_mm, 1)
            pe.sem_inc(b3_mm, 1)
            for s in (h1_mm, h2_mm, h3_mm):
                pe.sem_inc(s, 2)
            for u in range(2):
                pe.sem_inc(conv_mm[u], 1)
            pe.wait_ge(filled, N_FILL)
            pe.wait_ge(vstep, V_BAD)
            mm(p_bad, ones[0:RP, 0:RP], bad[0:RP, 1:2], start=True, stop=True).then_inc(bad_sum, 1)
            pe.wait_ge(flag_set, 1)
            flag = nc.tensor.value_load(fast_i[0:1, 0:1], min_val=0, max_val=1)

            def turn_rows(tables, n):
                for rb in range(RB):
                    k = n * RB + rb
                    if k >= 2:
                        pe.wait_ge(unturned, k - 1)
                    for a, table in enumerate(tables):
                        for h in range(TPG):
                            ins = nc.tensor.transpose(p_rows[k % 2][:, a, h, 0:RP], table[0:RP, rb, h * P:(h + 1) * P],
                                                      ident[0:RP, 0:RP])
                    ins.then_inc(turned, 1)

            pe.wait_ge(vstep, V_LOC)
            turn_rows((src_f, loc_f), 0)

            def degree_open(n):
                mm(p_deg[n], zero_b[:, :], zero_b[:, 0:NB], start=True, stop=False, skip_group_check=True)

            def degree_batch(n, it, k):
                b = n * DEG_ALL + k
                pe.wait_ge(deg_oh, it * BPI + (b + 1))
                for i in range(TPB):
                    ins = mm(p_deg[n], hlo[:, k % 2, i, :], hhi[:, k % 2, i, :], start=False, stop=False, skip_group_check=True)
                ins.then_inc(deg_mm, 1)

            def degree_close(n):
                mm(p_deg[n], zero_b[:, :], zero_b[:, 0:NB], start=False, stop=True, skip_group_check=True).then_inc(deg_end, 1)

            def degree_loop(n):
                with pe.Fori(0, ITERS) as it:
                    for k in range(BPI):
                        degree_batch(n, it, k)

            degree_open(0)
            degree_loop(0)
            degree_close(0)
            turn_rows((dst_f,), 1)
            degree_open(1)

            def group_products(psum, j, oh):
                for c in range(KD):
                    for h in range(TPG):
                        ins = mm(psum[:, c, :], gath[:, j, h, c * P:(c + 1) * P], oh[h], start=(h == 0), stop=(h == TPG - 1))
                return ins

            def aggregate(layer):
                with pe.If(flag):
                    with pe.Fori(0, ITERS) as it:
                        for j in range(GPI):
                            k, i = divmod(j * TPG, TPB)
                            if i == 0:
                                if layer == 0:
                                    degree_batch(1, it, k)
                                pe.wait_ge(oh_set, it * BPI + (layer * ITERS * BPI + k + 1))
                            pe.wait_ge(agg_add, it * GPI + (layer * ITERS * GPI + j + 1))
                            pe.wait_ge(rows_got[j], it * (16 * TPG) + 16 * TPG * (layer * ITERS + 1))
                            group_products(p_agg[j % AGG_SLOTS], j, [oneh[:, k, i + h, :] for h in range(TPG)]).then_inc(agg_mm, 1)
                with pe.Else():
                    if layer == 0:
                        degree_loop(1)
                    with pe.Fori(0, NG) as g:
                        pe.wait_ge(gen_rows, g * (16 * TPG) + 16 * TPG * (layer * NG + 1))
                        alone(pe, "pe")
                        with pe.Fori(0, NW) as w:
                            pe.wait_ge(gen_oh, g * NW + w + (layer * NG * NW + 1))
                            group_products(p_agg[0], 0, [oneh[:, 0, h, :] for h in range(TPG)]).then_inc(gen_mm, 1)

            def conv(layer, u, uses, psum):
                pe.wait_ge(staged[u], uses + 1)
                for k in range(KD):
                    ins = mm(psum, stage[:, u, k, :], cw[:, layer, k, :], start=(k == 0), stop=(k == KD - 1))
                ins.then_inc(conv_mm[u], 1)

            aggregate(0)
            degree_close(1)
            pe.wait_ge(consts_in, 16 * N_CONST)
            with pe.Fori(0, HB) as i:
                for u in range(2):
                    pe.wait_ge(conv_ev[u], i + 1)
                    conv(0, u, i, p_conv1[u])
            aggregate(1)
            pe.wait_ge(we_in, 16 * 3 * NE)

            def body(q, u, front, experts):
                m = 2 * q + u
                v = 1 - u

                def bank_free(what, e):
                    was, e0, back = exp_before(what, e)
                    done, credit = {"l1": (h1_set, 2), "l2": (h2_set, 2), "l3": (h3_ev, 3)}[was]
                    pe.wait_ge(done, (m - 1) * NE + (e0 + 1 + credit - back * NE))

                for what, e in expert_order():
                    k = (m - 1) * NE + e
                    if what == "l1" and experts:
                        if e == 0:
                            pe.wait_ge(xnT_set, m)
                        bank_free(what, e)
                        psum = exp_bank(what, e, v).rearrange("p (k n) -> p k n", k=KD)
                        for c in range(KD):
                            for i in range(KD):
                                ins = mm(psum[:, c, :], we[:, 0, e, i, c * P:(c + 1) * P], xnT[:, v, i, :],
                                         start=(i == 0), stop=(i == KD - 1))
                        ins.then_inc(h1_mm, 1)
                    if what == "l2" and experts:
                        pe.wait_ge(h1_set, k + 3)
                        bank_free(what, e)
                        psum = exp_bank(what, e, v).rearrange("p (k n) -> p k n", k=KD)
                        for c in range(KD):
                            for i in range(KD):
                                ins = mm(psum[:, c, :], we[:, 1, e, i, c * P:(c + 1) * P], h1T[:, e % 2, i, :],
                                         start=(i == 0), stop=(i == KD - 1))
                        ins.then_inc(h2_mm, 1)
                    if what == "l3" and experts:
                        pe.wait_ge(h2_set, k + 3)
                        bank_free(what, e)
                        for i in range(KD):
                            ins = mm(exp_bank(what, e, v), h2T[:, e % 2, i, :], we[:, 2, e, i, :], start=(i == 0), stop=(i == KD - 1))
                        ins.then_inc(h3_mm, 1)
                    if what == "gT" and experts:
                        pe.wait_ge(gate_set, m)
                        nc.tensor.transpose(p_gT, gate[:, v, :], ident[:, :]).then_inc(gT_mm, 1)
                    if what == "b3" and experts:
                        pe.wait_ge(gT_set, m)
                        if front:
                            pe.wait_ge(conv_ev[u], q + (HB + 2))
                        else:
                            pe.wait_ge(acc_init, m)
                        mm(p_b3, gateT[:, :], eb3[:, :], start=True, stop=True).then_inc(b3_mm, 1)
                    if what == "conv" and front:
                        need(pe, rh_set, m)
                        conv(1, u, q + HB, p_conv)
                    if what == "tr" and front:
                        pe.wait_ge(xn_set, m + 1)
                        need(pe, xnT_set, m)
                        for i in range(KD):
                            ins = nc.tensor.transpose(p_xnT[:, i, :], xn[:, i * P:(i + 1) * P], ident[:, :])
                        ins.then_inc(xnT_mm, 1)
                    if what == "rh" and front:
                        pe.wait_ge(xnT_set, m + 1)
                        if experts:
                            pe.wait_ge(acc_init, m + 1)
                        for i in range(KD):
                            ins = mm(p_rh, rw1[:, i, :], xnT[:, u, i, :], start=(i == 0), stop=(i == KD - 1))
                        ins.then_inc(rh_mm, 1)
                    if what == "lg" and front:
                        pe.wait_ge(rh_set, m + 1)
                        mm(p_lg, rhT[:, :], rw2[:, :], start=True, stop=True).then_inc(lg_mm, 1)

            bodies(pe, body)

        @block.vector
        def _(dve):
            ve = nc.vector
            dve.sem_inc(agg_add, AGG_SLOTS)
            dve.sem_inc(gen_add, 1)
            dve.sem_inc(gen_loc, 1)
            dve.sem_inc(hb_set, 1)
            dve.sem_inc(acc_init, 1)
            dve.sem_inc(h3_ev, 3)
            for u in range(2):
                dve.sem_inc(conv_ev[u], 1)
            v = Steps(vstep)

            def step(ins):
                v.inc(ins)
                dve.wait_ge(vstep, v.now())

            dve.wait_ge(filled, N_FILL)
            ve.memset(prob[:, :], -1.0)
            step(ve.tensor_copy(iota[:, :], iota_i[:, :]))
            step(ve.tensor_copy(iota_pf[:, :], iota_p[:, :]))
            step(ve.tensor_scalar(ident[:, :], iota[:, :], iota_pf[:, 0:1], None, ALU.is_equal))
            step(ve.tensor_scalar(iota_hi[:, :], iota[:, 0:NB], float(P), None, ALU.mult))
            dve.wait_ge(rows_in, 16 * N_ROWS)
            step(ve.tensor_copy(src_f[0:RP], src_i[0:RP]))
            step(ve.tensor_copy(dst_f[0:RP], dst_i[0:RP]))
            step(ve.tensor_reduce(base_f[0:RP, :], dst_f[0:RP], X, ALU.min))
            step(ve.tensor_scalar(base_f[0:RP, :], base_f[0:RP, :], float(N - 1), None, ALU.min))

            def relative():
                step(ve.tensor_tensor(loc_f[0:RP], dst_f[0:RP], base_f[0:RP, :].unsqueeze(2).to_broadcast([RP, RB, EPG]),
                                      ALU.subtract))

            relative()
            spans = rows[0:RP, 0, :, :]
            step(ve.scalar_tensor_tensor(spans, loc_f[0:RP], FAR / 2, loc_f[0:RP], ALU.is_lt, ALU.mult))
            step(ve.tensor_reduce(bad[0:RP, 0:1], spans.rearrange("p b e -> p (b e)"), X, ALU.max))
            step(ve.tensor_scalar(bad[0:RP, 1:2], bad[0:RP, 0:1], float(WIN), None, ALU.is_ge))
            assert v.n == V_BAD
            dve.wait_ge(bad_sum, 1)
            step(ve.tensor_scalar(fast[0:RP, :], p_bad, 0.5, None, ALU.is_lt))
            ve.tensor_copy(fast_i[0:RP, :], fast[0:RP, :]).then_inc(flag_set, 1)
            step(ve.tensor_scalar(base_f[0:RP, :], base_f[0:RP, :], fast[0:RP, 0:1], None, ALU.mult))
            ve.tensor_copy(base_i[0:RP, :], base_f[0:RP, :]).then_inc(flag_set, 1)
            relative()
            assert v.n == V_LOC
            dve.wait_ge(flag_set, 2)
            flag = ve.value_load(fast_i[0:1, 0:1], min_val=0, max_val=1)

            def rsqrt(step, y, x, t):
                step(ve.tensor_scalar(t.bitcast(I32), x.bitcast(I32), 1, None, ALU.logical_shift_right))
                step(ve.tensor_scalar(y.bitcast(I32), t.bitcast(I32), -1.0, float(0x5F3759DF), ALU.mult, ALU.add))
                for _ in range(3):
                    step(ve.tensor_tensor(t, y, y, ALU.mult))
                    step(ve.scalar_tensor_tensor(t, t, -0.5, x, ALU.mult, ALU.mult))
                    step(ve.scalar_tensor_tensor(y, t, 1.5, y, ALU.add, ALU.mult))

            def inverse_root(scale, n):
                step(ve.tensor_scalar(deg[:, :], p_deg[n], 1.0, None, ALU.max))
                rsqrt(step, scale[:, :], deg[:, :], dtmp[:, :])

            def unturn(tables, n):
                for rb in range(RB):
                    k = n * RB + rb
                    dve.wait_ge(turned, k + 1)
                    for a, table in enumerate(tables):
                        ins = ve.tensor_copy(table.rearrange("p (g h) -> p g h", h=TPG)[:, rb * RP:(rb + 1) * RP, :],
                                             p_rows[k % 2][:, a, :, 0:RP].rearrange("p h n -> p n h"))
                    ins.then_inc(unturned, 1)
                dve.wait_ge(unturned, (n + 1) * RB)

            def split_ids():
                lo_i = loT.bitcast(I32)
                step(ve.tensor_copy(lo_i, hiT))
                step(ve.tensor_scalar(lo_i, lo_i, P - 1, None, ALU.bitwise_and))
                step(ve.tensor_copy(loT, lo_i))
                step(ve.tensor_tensor(hiT, hiT, loT, ALU.subtract))

            unturn((hiT, locT[:, :]), 0)
            step(ve.tensor_scalar(idxT[:, :], hiT, float(N - 1), None, ALU.min))
            assert v.n == V_IDX
            split_ids()

            def degree_batch(n, it, k):
                b = n * DEG_ALL + k
                dve.wait_ge(deg_mm, it * BPI + (b + 1))
                t0 = it * TPI + k * TPB
                ve.tensor_tensor(hlo[:, k % 2, :, :], iota[:, :].unsqueeze(1).to_broadcast([P, TPB, P]),
                                 loT[:, bass.ds(t0, TPB)].unsqueeze(2).to_broadcast([P, TPB, P]), ALU.is_equal)
                ve.tensor_tensor(hhi[:, k % 2, :, :], iota_hi[:, :].unsqueeze(1).to_broadcast([P, TPB, NB]),
                                 hiT[:, bass.ds(t0, TPB)].unsqueeze(2).to_broadcast([P, TPB, NB]), ALU.is_equal).then_inc(deg_oh, 1)

            def degree_loop(n):
                with dve.Fori(0, ITERS) as it:
                    for k in range(BPI):
                        degree_batch(n, it, k)

            degree_loop(0)
            dve.wait_ge(deg_end, 1)
            inverse_root(out_s, 0)
            dve.wait_ge(x_in, 16 * (NXC + 1))
            with dve.Fori(0, NXC) as c:
                v.enter(c, XC)
                for i in range(XC):
                    b = c * XC + i
                    v.inc(ve.bn_stats(stat[:, bass.ds(b, 1), :].rearrange("p a s -> p (a s)"),
                                      xbig[:, bass.ds(b, 1), :].rearrange("p a d -> p (a d)")))
            v.leave(NXC)
            dve.wait_ge(vstep, v.now())
            step(ve.tensor_tensor(mean[:, :], stat[:, :, 1], stat[:, :, 4], ALU.add))
            step(ve.tensor_scalar(mean[:, :], mean[:, :], 0.5, None, ALU.mult))
            step(ve.tensor_tensor(mdif[:, :], stat[:, :, 1], mean[:, :], ALU.subtract))
            step(ve.tensor_tensor(mdif[:, :], mdif[:, :], mdif[:, :], ALU.mult))
            step(ve.tensor_tensor(rstd[:, :], stat[:, :, 2], stat[:, :, 5], ALU.add))
            step(ve.scalar_tensor_tensor(rstd[:, :], rstd[:, :], 1.0 / D, mdif[:, :], ALU.mult, ALU.add))
            step(ve.tensor_scalar(mdif[:, :], rstd[:, :], 1e-5, None, ALU.add))
            rsqrt(step, rstd[:, :], mdif[:, :], dtmp[:, :])
            step(ve.tensor_tensor(rstd[:, :], rstd[:, :], out_s[:, :], ALU.mult))
            with dve.Fori(0, NXC) as c:
                for i in range(XC):
                    b = c * XC + i
                    xb = xbig[:, bass.ds(b, 1), :].rearrange("p a d -> p (a d)")
                    ve.tensor_scalar(xb, xb, mean[:, bass.ds(b, 1)], rstd[:, bass.ds(b, 1)],
                                     ALU.subtract, ALU.mult).then_inc(normed, 1)
            unturn((hiT,), 1)
            split_ids()
            dve.wait_ge(table_out, 16 * (NXC + 1))
            ve.memset(aggT[:, 0:KD - 1, :], 0.0).then_inc(agg_zero, 1)
            dve.wait_ge(agg_zero, 2)
            dve.wait_ge(bases_in, 16)

            def add_group(where, psum, done):
                ve.tensor_tensor(aggT[:, :, where], aggT[:, :, where], psum, ALU.add).then_inc(done, 1)

            def one_hot(oh, local, tiles):
                return ve.tensor_tensor(oh, iota[:, 0:WIN].unsqueeze(1).to_broadcast([P, tiles, WIN]),
                                        local.unsqueeze(2).to_broadcast([P, tiles, WIN]), ALU.is_equal)

            def aggregate(layer):
                with dve.If(flag):
                    with dve.Fori(0, ITERS) as it:
                        left = ahead(dve, it, ITERS)

                        def batch(k):
                            dve.wait_ge(agg_mm, it * GPI + (layer * ITERS * GPI + (k + 1) * (TPB // TPG)))
                            col = left * TPI + k * TPB
                            one_hot(oneh[:, k, :, :], locT[:, bass.ds(col, TPB)], TPB).then_inc(oh_set, 1)
                            if layer == 0:
                                degree_batch(1, it, k)

                        def add(j):
                            base = ve.value_load(base_l[0:1, bass.ds(left * GPI + j, 1)], min_val=0, max_val=N - 1)
                            done = it * GPI + (layer * ITERS * GPI + j)
                            dve.wait_ge(agg_mm, done + (GPI + 1))
                            dve.wait_ge(agg_add, done + AGG_SLOTS)
                            add_group(bass.ds(base, WIN), p_agg[j % AGG_SLOTS], agg_add)

                        batch(0)
                        for k in range(BPI):
                            if k + 1 < BPI:
                                batch(k + 1)
                            for j in range(k * (TPB // TPG), (k + 1) * (TPB // TPG)):
                                add(j)
                    dve.wait_ge(agg_add, (layer + 1) * ITERS * GPI + AGG_SLOTS)
                with dve.Else():
                    if layer == 0:
                        degree_loop(1)
                    with dve.Fori(0, NG) as g:
                        n0 = g * NW + layer * NG * NW
                        dve.wait_ge(gen_add, n0 + 1)
                        dve.wait_ge(gen_loc, g * (NW + 1) + (layer * NG * (NW + 1) + 1))
                        ve.tensor_copy(locw[:, :], locT[:, bass.ds(g * TPG, TPG)]).then_inc(gen_loc, 1)
                        with dve.Fori(0, NW) as w:
                            dve.wait_ge(gen_loc, g * (NW + 1) + w + (layer * NG * (NW + 1) + 2))
                            one_hot(oneh[:, 0, 0:TPG, :], locw[:, :], TPG).then_inc(gen_oh, 1)
                            dve.wait_ge(gen_oh, n0 + w + 1)
                            ve.tensor_scalar(locw[:, :], locw[:, :], float(-WIN), None, ALU.add).then_inc(gen_loc, 1)
                            dve.wait_ge(gen_mm, n0 + w + 2)
                            add_group(bass.ds(w * WIN, WIN), p_agg[0], gen_add)
                            dve.wait_ge(gen_add, n0 + w + 2)
                            alone(dve, "dve")
                dve.sem_inc(agg_done, 1)

            aggregate(0)
            dve.wait_ge(deg_end, 2)
            inverse_root(in_s, 1)
            dve.wait_ge(consts_in, 16 * N_CONST)

            def conv_out(layer, psum, left, u, uses):
                dve.wait_ge(conv_mm[u], uses + 2)
                ve.scalar_tensor_tensor(tb[:, u, :], psum, in_s[:, bass.ds(left * 2 + (1 - u), 1)], cb[:, layer, :],
                                        ALU.mult, ALU.add).then_inc(conv_ev[u], 1)
                dve.wait_ge(conv_ev[u], uses + 2)

            with dve.Fori(0, HB) as i:
                left = ahead(dve, i, HB)
                for u in range(2):
                    dve.wait_ge(hb_set, 2 * i + (u + 1))
                    conv_out(0, p_conv1[u], left, u, i)
                    dve.wait_ge(hb_free[u], i + 1)
                    ve.tensor_scalar(hb[:, u, :], tb[:, u, :], 0.0, out_s[:, bass.ds(left * 2 + (1 - u), 1)],
                                     ALU.max, ALU.mult).then_inc(hb_set, 1)
            for u in range(2):
                dve.wait_ge(cleared[u], HB)
            aggregate(1)

            s = Steps(bstep)

            def bs(ins):
                s.inc(ins)
                dve.wait_ge(bstep, s.now())

            def body(q, u, front, experts):
                m = 2 * q + u
                w = 1 - u
                if front:
                    conv_out(1, p_conv, ahead(dve, q, HB), u, q + HB)
                    dve.wait_ge(xin_in[u], q * 16 + 16)
                    ve.scalar_tensor_tensor(xr[:, u, :], tb[:, u, :], 0.0, xin[:, u, :], ALU.max, ALU.add).then_inc(xr_set, 1)
                    dve.wait_ge(xr_set, m + 1)
                    bs(ve.bn_stats(st6[:, :], xr[:, u, :]))
                    alone(dve, "dve")
                    bs(ve.bn_aggr(mv[:, :], st6[:, :]))
                    bs(ve.tensor_scalar(rv[:, :], mv[:, 1:2], 1e-5, None, ALU.add))
                    rsqrt(bs, rs[:, :], rv[:, :], rt[:, :])
                    need(dve, xnT_mm, m)
                    ve.tensor_scalar(xn[:, :], xr[:, u, :], mv[:, 0:1], rs[:, 0:1], ALU.subtract, ALU.mult).then_inc(xn_set, 1)
                    dve.wait_ge(xn_set, m + 1)
                if experts:
                    dve.wait_ge(acc_free[w], q + u)
                    dve.wait_ge(b3_mm, m + 1)
                    ve.tensor_tensor(acc[:, w, :], xr[:, w, :], p_b3, ALU.add).then_inc(acc_init, 1)
                    dve.wait_ge(acc_init, m + 1)
                    dve.wait_ge(gate_set, m)

                def add_expert(e):
                    k = (m - 1) * NE + e
                    dve.wait_ge(h3_mm, k + 3)
                    if e:
                        dve.wait_ge(h3_ev, k + 3)
                    ve.scalar_tensor_tensor(acc[:, w, :], exp_bank("l3", e, w), gate[:, w, e:e + 1], acc[:, w, :],
                                            ALU.mult, ALU.add).then_inc(h3_ev, 1)

                if experts:
                    for e in range(NE - 2):
                        add_expert(e)
                if front:
                    dve.wait_ge(lg_mm, m + 1)
                    bs(ve.tensor_tensor(lg[:, :], p_lg, rb2[:, :], ALU.add))
                    ve.tensor_reduce(lmax[:, :], lg[:, :], X, ALU.max, negate=True).then_inc(lmax_set, 1)
                if experts:
                    add_expert(NE - 2)
                if front:
                    dve.wait_ge(pe_set, m + 1)
                    bs(ve.reciprocal(psumr[:, :], psumr[:, :]))
                    bs(ve.tensor_scalar(prob[:, 0:NE], pexp[:, :], psumr[:, 0:1], None, ALU.mult))
                    alone(dve, "dve")
                    bs(ve.max(top[:, :], prob[:, :]))
                    ve.tensor_tensor(w12[:, 0:1], top[:, 1:2], top[:, 0:1], ALU.subtract).then_inc(wd_set, 1)
                    bs(ve.max_index(topi[:, :], top[:, :], prob[:, :]))
                    bs(ve.tensor_copy(topf[:, :], topi[:, :]))
                if experts:
                    add_expert(NE - 1)
                if front:
                    dve.wait_ge(wx_set, m + 1)
                    bs(ve.tensor_scalar(w12[:, 2:3], w12[:, 1:2], 1.0, None, ALU.add))
                    bs(ve.reciprocal(w12[:, 3:4], w12[:, 2:3]))
                    bs(ve.tensor_tensor(w12[:, 2:3], w12[:, 1:2], w12[:, 3:4], ALU.mult))
                    bs(ve.tensor_scalar(gt2[:, :], iota[:, 0:NE], topf[:, 1:2], w12[:, 2:3], ALU.is_equal, ALU.mult))
                    bs(ve.tensor_scalar(gate[:, u, :], iota[:, 0:NE], topf[:, 0:1], w12[:, 3:4], ALU.is_equal, ALU.mult))
                    ve.tensor_tensor(gate[:, u, :], gate[:, u, :], gt2[:, :], ALU.add).then_inc(gate_set, 1)

            PER_FRONT = 3 + 11 + 1 + 5 + 5
            body(0, 0, True, False)
            with dve.Fori(0, HB - 1) as i:
                s.enter(i, 2 * PER_FRONT)
                body(i, 1, True, True)
                body(i + 1, 0, True, True)
            s.leave(HB - 1)
            body(HB - 1, 1, True, True)
            body(HB, 0, False, True)


_INS = ["x", "src", "dst", "L0_gnn_W1", "L0_gnn_b1", "L0_gnn_W2", "L0_gnn_b2", "L0_ffn_router_w1", "L0_ffn_router_b1",
        "L0_ffn_router_w2", "L0_ffn_router_b2", "L0_ffn_expert_w1", "L0_ffn_expert_b1", "L0_ffn_expert_w2",
        "L0_ffn_expert_b2", "L0_ffn_expert_w3", "L0_ffn_expert_b3"]


def kernel(**inputs):
    import numpy as _np
    import concourse.bacc as _bacc
    from concourse import mybir as _mybir
    from concourse.bass_utils import run_bass_kernel_spmd as _run

    nc = _bacc.Bacc("TRN2", target_bir_lowering=False, num_devices=1)
    arrays, args = {}, {}
    for name in _INS:
        a = _np.ascontiguousarray(inputs[name])
        arrays[f"in_{name}_dram"] = a
        args[name] = nc.dram_tensor(f"in_{name}_dram", a.shape, _mybir.dt.from_np(a.dtype), kind="ExternalInput").ap()
    out = nc.dram_tensor("out_dram", arrays["in_x_dram"].shape, _mybir.dt.float32, kind="ExternalOutput").ap()
    gnn_experts(nc, args, out)
    r = _run(nc, [arrays], core_ids=[0])
    return r.results[0]["out_dram"]
```

```python
from contextlib import ExitStack

import concourse.bass as bass
from concourse import mybir

P = 128
WIN = 64
TPG = 2
EPG = TPG * P
GPI = 8
TPI = GPI * TPG
TPB = 4
BPI = TPI // TPB
CHUNK = TPI // 2
LAG = 1
AGG_SLOTS = 2
FAR = 1.0e6

F32 = mybir.dt.float32
BF16 = mybir.dt.bfloat16
I32 = mybir.dt.int32
U32 = mybir.dt.uint32
ALU = mybir.AluOpType
ACT = mybir.ActivationFunctionType
X = mybir.AxisListType.X


V_BAD = 19
V_LOC = 22
V_IDX = 23


class Steps:

    def __init__(self, sem, credit=0):
        self.sem, self.n, self.it, self.per, self.start = sem, credit, None, 0, 0

    def inc(self, ins):
        ins.then_inc(self.sem, 1)
        self.n += 1

    def enter(self, it, per):
        self.it, self.per, self.start = it, per, self.n

    def leave(self, trips):
        assert self.n - self.start == self.per, (self.n - self.start, self.per)
        self.n, self.it = self.start + self.per * trips, None

    def now(self, ahead=0):
        n = self.n + ahead
        return n if self.it is None else self.it * self.per + n


def gnn_experts(nc, t, out):
    N, D = t["x"].shape
    E = t["src"].shape[0]
    NE, _, H = t["L0_ffn_expert_w1"].shape
    RH = t["L0_ffn_router_w1"].shape[1]
    assert D == 2 * P and H == 2 * P and RH == P and NE <= 8
    KD = D // P
    NB = -(-N // P)
    LAST = N - (NB - 1) * P
    ITERS = -(-E // (EPG * GPI))
    NG = ITERS * GPI
    NT = NG * TPG
    FULLG, REST = E // EPG, E % EPG
    RB = -(-NG // P)
    RP = NG // RB
    assert NG % RB == 0 and RP <= P and GPI * 16 == P
    assert ITERS == NB
    NW = -(-N // WIN)
    COLS = N + WIN
    assert COLS >= NB * P and COLS >= NW * WIN and NB % 2 == 0
    XC = 7
    assert NB % (2 * XC) == 0 and 2 * XC <= TPI
    NXC = NB // XC

    h_tab = [nc.dram_tensor(f"table{n + 1}", (N, D), F32, kind="Internal").ap() for n in range(2)]
    base_dram = nc.dram_tensor("base_list", (NG,), I32, kind="Internal").ap()

    ctx = ExitStack()
    with ctx:
        ctx.enter_context(nc.allow_non_contiguous_dma(reason="small bias columns and group bases"))

        def sb(name, shape, dt=F32):
            return ctx.enter_context(nc.sbuf_tensor(name, shape, dt))

        def sem(name):
            return ctx.enter_context(nc.semaphore(name))

        big = sb("big", [P, max(NB * D, KD * COLS)])
        xbig = big[:, 0:NB * D].rearrange("p (b d) -> p b d", d=D)
        aggT = big[:, 0:KD * COLS].rearrange("p (k n) -> p k n", k=KD)
        WE = 3 * NE * KD * H
        late = sb("late", [P, max(WE, 4 * RB * EPG)])
        rows = late[:, 0:4 * RB * EPG].rearrange("p (a b e) -> p a b e", a=4, e=EPG)
        src_i, dst_i = rows[:, 0, :, :].bitcast(I32), rows[:, 1, :, :].bitcast(I32)
        src_f, dst_f = rows[:, 2, :, :], rows[:, 3, :, :]
        loc_f = rows[:, 1, :, :]
        we = late[:, 0:WE].rearrange("p (l e k h) -> p l e k h", l=3, e=NE, k=KD)
        idxT = sb("idxT", [P, TPI + NT], I32)
        locT = sb("locT", [P, NT])
        OH = TPB * (P + NB)
        work = sb("work", [P, max(2 * NT + OH, 14 * D)])
        hiT, loT = work[:, 0:NT], work[:, NT:2 * NT]
        onehots = work[:, 2 * NT:2 * NT + OH].bitcast(BF16).rearrange("p (b n) -> p b n", b=2)
        hlo = onehots[:, :, 0:TPB * P].rearrange("p b (t n) -> p b t n", t=TPB)
        hhi = onehots[:, :, TPB * P:].rearrange("p b (t n) -> p b t n", t=TPB)
        wrows = work[:, 0:14 * D].rearrange("p (a d) -> p a d", d=D)
        xr = wrows[:, 0:2, :]
        acc = wrows[:, 2:4, :]
        xnT = wrows[:, 4:6, :].rearrange("p b (k n) -> p b k n", k=KD)
        h1T = wrows[:, 6:8, :].rearrange("p b (k n) -> p b k n", k=KD)
        h2T = wrows[:, 8:10, :].rearrange("p b (k n) -> p b k n", k=KD)
        xn = wrows[:, 10, :]
        stage = wrows[:, 11:13, :].rearrange("p b (k n) -> p b k n", k=KD)
        gateT = wrows[0:NE, 13, 0:P]
        base_f = sb("base_f", [P, RB])
        gid_i = sb("gid_i", [P, RB], I32)
        bound = sb("bound", [P, RB])
        reach = sb("reach", [P, RB])
        base_i = sb("base_i", [P, RB], I32)
        base_l = sb("base_l", [1, NG], I32)
        bad = sb("bad", [P, 2])
        fast = sb("fast", [P, 1])
        fast_i = sb("fast_i", [P, 1], I32)
        iota_i = sb("iota_i", [P, P], I32)
        iota_p = sb("iota_p", [P, 1], I32)
        iota_pf = sb("iota_pf", [P, 1])
        iota = sb("iota", [P, P])
        iota_hi = sb("iota_hi", [P, NB])
        ident = sb("ident", [P, P])
        ones = sb("ones", [P, P])
        zero_b = sb("zero_b", [P, P], BF16)
        zeros = sb("zeros", [P, D])
        cw = sb("cw", [P, 2, KD, D])
        cb = sb("cb", [P, 2, D])
        rw1 = sb("rw1", [P, KD, RH])
        rb1 = sb("rb1", [P, 1])
        rw2 = sb("rw2", [P, NE])
        rb2 = sb("rb2", [P, NE])
        eb = sb("eb", [P, 2, NE, KD])
        eb3 = sb("eb3", [NE, D])
        out_s = sb("out_s", [P, NB])
        in_s = sb("in_s", [P, NB])
        deg = sb("deg", [P, NB])
        dtmp = sb("dtmp", [P, NB])
        mean = sb("mean", [P, NB])
        mdif = sb("mdif", [P, NB])
        rstd = sb("rstd", [P, NB])
        idx = [sb(f"idx{n}", [P, CHUNK], I32) for n in range(2)]
        gath = sb("gath", [P, GPI, TPG, D])
        hb = gath[:, :, :, :].rearrange("p g t d -> p (g t) d")[:, 0:2 * XC, :].rearrange(
            "p (a b) d -> p a b d", a=2)
        stat = gath[:, :, :, :].rearrange("p g t d -> p (g t d)")[:, 0:NB * 6].rearrange("p (b s) -> p b s", s=6)
        oneh = sb("oneh", [P, BPI, TPB, WIN])
        locw = sb("locw", [P, TPG])
        tb = sb("tb", [P, 2, D])
        xin = sb("xin", [P, 2, D])
        st6 = sb("st6", [P, 6])
        mv = sb("mv", [P, 2])
        rs, rv, rt = (sb(n, [P, 1]) for n in ("rs", "rv", "rt"))
        rhT = sb("rhT", [P, P])
        lg = sb("lg", [P, NE])
        lmax = sb("lmax", [P, 1])
        pexp = sb("pexp", [P, NE])
        psumr = sb("psumr", [P, 1])
        prob = sb("prob", [P, 8])
        top = sb("top", [P, 8])
        topi = sb("topi", [P, 8], U32)
        topf = sb("topf", [P, 8])
        w12 = sb("w12", [P, 4])
        gate = sb("gate", [P, 2, NE])
        gt2 = sb("gt2", [P, NE])

        def bank(name):
            return ctx.enter_context(nc.psum_tensor(name, [P, 512], F32))

        b_agg = [bank(f"b_agg{n}") for n in range(AGG_SLOTS)]
        b_front = [bank(f"b_front{n}") for n in range(2)]
        b_exp = [bank(f"b_exp{n}") for n in range(4)]
        p_agg = [b[:, 0:KD * WIN].rearrange("p (k w) -> p k w", k=KD) for b in b_agg]
        p_conv1 = [b[:, 0:D] for b in b_front]
        p_conv = b_front[0][:, 0:D]
        p_b3 = b_front[0][:, D:2 * D]
        p_rh = b_front[0][:, 0:P]
        p_gT = b_front[1][0:NE, 0:P]
        p_xnT = b_front[1][:, 0:D].rearrange("p (k n) -> p k n", k=KD)
        p_lg = b_front[1][:, D:D + NE]
        p_exp = [b[:, 0:D] for b in b_exp]
        p_deg = [b[:, 0:NB] for b in b_exp[0:2]]
        p_rows = [b[:, :].rearrange("p (a h n) -> p a h n", a=2, h=TPG) for b in b_front]
        p_bad = b_exp[2][0:RP, 0:1]

        filled = sem("filled")
        rows_in = sem("rows_in")
        consts_in = sem("consts_in")
        x_in = sem("x_in")
        vstep = sem("vstep")
        bad_sum = sem("bad_sum")
        flag_set = sem("flag_set")
        turned = sem("turned")
        unturned = sem("unturned")
        deg_oh = sem("deg_oh")
        deg_mm = sem("deg_mm")
        deg_end = sem("deg_end")
        bases_out = sem("bases_out")
        bases_in = sem("bases_in")
        normed = sem("normed")
        table_out = sem("table_out")
        agg_zero = sem("agg_zero")
        idx_set = [sem(f"idx_set{n}") for n in range(2)]
        rows_got = [sem(f"rows_got{n}") for n in range(GPI)]
        oh_set = sem("oh_set")
        agg_mm = sem("agg_mm")
        agg_add = sem("agg_add")
        gen_idx = sem("gen_idx")
        gen_rows = sem("gen_rows")
        gen_oh = sem("gen_oh")
        gen_mm = sem("gen_mm")
        gen_add = sem("gen_add")
        gen_loc = sem("gen_loc")
        passed = {n: sem(f"passed_{n}") for n in ("pool", "pe", "dve", "sp")}
        agg_done = sem("agg_done")
        staged = [sem(f"staged{n}") for n in range(2)]
        cleared = [sem(f"cleared{n}") for n in range(2)]
        conv_mm = [sem(f"conv_mm{n}") for n in range(2)]
        conv_ev = [sem(f"conv_ev{n}") for n in range(2)]
        hb_set = sem("hb_set")
        hb_out = [sem(f"hb_out{n}") for n in range(2)]
        hb_end = sem("hb_end")
        hb_free = [sem(f"hb_free{n}") for n in range(2)]
        we_in = sem("we_in")
        xin_in = [sem(f"xin_in{n}") for n in range(2)]
        bstep = sem("bstep")
        xr_set = sem("xr_set")
        xn_set = sem("xn_set")
        xnT_mm = sem("xnT_mm")
        xnT_set = sem("xnT_set")
        rh_mm = sem("rh_mm")
        rh_set = sem("rh_set")
        lg_mm = sem("lg_mm")
        lmax_set = sem("lmax_set")
        pe_set = sem("pe_set")
        wd_set = sem("wd_set")
        wx_set = sem("wx_set")
        gate_set = sem("gate_set")
        gT_mm = sem("gT_mm")
        gT_set = sem("gT_set")
        b3_mm = sem("b3_mm")
        h1_mm = sem("h1_mm")
        h2_mm = sem("h2_mm")
        h3_mm = sem("h3_mm")
        h1_set = sem("h1_set")
        h2_set = sem("h2_set")
        acc_init = sem("acc_init")
        h3_ev = sem("h3_ev")
        acc_free = [sem(f"acc_free{n}") for n in range(2)]
        out_st = [sem(f"out_st{n}") for n in range(2)]

        block = ctx.enter_context(nc.Block())

        HB = NB // 2
        N_CONST = 2 * 2 + 4 + 2 * NE + 1
        N_ROWS = 2 * ((1 if FULLG // RP else 0) + (1 if FULLG % RP else 0) + (1 if REST else 0))
        N_FILL = 8
        DEG_ALL = ITERS * BPI

        def need(eng, semaphore, value):
            if not isinstance(value, int) or value > 0:
                eng.wait_ge(semaphore, value)

        def alone(eng, name):
            eng.sem_inc(passed[name], 1)

        def column(left, u):
            return left * (2 * P) + (1 - u) * P

        def expert_order():
            return [("l1", 0), ("l1", 1), ("gT", 0), ("conv", 0), ("l2", 0), ("l1", 2), ("l2", 1), ("b3", 0), ("l3", 0),
                    ("l1", 3), ("l2", 2), ("l3", 1), ("tr", 0), ("l1", 4), ("l2", 3), ("l3", 2), ("rh", 0),
                    ("l1", 5), ("l2", 4), ("l3", 3), ("lg", 0), ("l2", 5), ("l3", 4), ("l3", 5)]

        OUTPUTS = [x for x in expert_order() if x[0] in ("l1", "l2", "l3")]

        def exp_bank(what, e, v):
            return p_exp[(OUTPUTS.index((what, e)) + v * 3 * NE) % 4]

        def exp_before(what, e):
            at = OUTPUTS.index((what, e)) - 4
            return (*OUTPUTS[at], 1 if at < 0 else 0)

        def ahead(eng, q, n):
            return n - 1 - q if isinstance(q, int) else eng.snap(q * (-1) + (n - 1), min_val=0, max_val=n - 1)

        def bodies(eng, body):
            body(0, 0, True, False)
            with eng.Fori(0, HB - 1) as i:
                body(i, 1, True, True)
                body(i + 1, 0, True, True)
            body(HB - 1, 1, True, True)
            body(HB, 0, False, True)

        def fused(eng, body, all_added=None):
            body(0, 0, False, False, 0)
            body(0, 0, True, False, 1)
            with eng.Fori(0, HB - 1) as i:
                body(i, 1, True, True, 2 * i + 2)
                body(i + 1, 0, True, True, 2 * i + 3)
            if all_added:
                eng.wait_ge(agg_add, all_added)
            body(HB - 1, 1, True, True)
            body(HB, 0, False, True)

        @block.sync
        def _(sp):
            sp.wait_ge(filled, 1)
            whole, part = FULLG // RP, FULLG % RP
            for name, rt in (("src", src_i), ("dst", dst_i)):
                if whole:
                    sp.dma_start(rt[0:RP, 0:whole, :], t[name][0:whole * RP * EPG].rearrange(
                        "(b p e) -> p b e", p=RP, e=EPG)).then_inc(rows_in, 16)
                if part:
                    sp.dma_start(rt[0:part, whole, :], t[name][whole * RP * EPG:FULLG * EPG].rearrange(
                        "(p e) -> p e", e=EPG)).then_inc(rows_in, 16)
                if REST:
                    sp.dma_start(rt[part:part + 1, whole, 0:REST], t[name][FULLG * EPG:E].rearrange(
                        "(p e) -> p e", p=1)).then_inc(rows_in, 16)
            for c in range(NXC):
                last = NB - 1 if c == NXC - 1 else (c + 1) * XC
                sp.dma_start(xbig[:, c * XC:last, :], t["x"][c * XC * P:last * P, :].rearrange(
                    "(b q) d -> q b d", q=P)).then_inc(x_in, 16)
            sp.dma_start(xbig[0:LAST, NB - 1, :], t["x"][(NB - 1) * P:N, :]).then_inc(x_in, 16)
            for n in range(2):
                sp.dma_start(cw[:, n, :, :], t[f"L0_gnn_W{n + 1}"].rearrange("(k p) d -> p k d", p=P)).then_inc(consts_in, 16)
                sp.dma_start(cb[:, n, :], t[f"L0_gnn_b{n + 1}"].partition_broadcast(P)).then_inc(consts_in, 16)
            sp.dma_start(rw1[:, :, :], t["L0_ffn_router_w1"].rearrange("(k p) h -> p k h", p=P)).then_inc(consts_in, 16)
            sp.dma_start(rb1[:, :], t["L0_ffn_router_b1"].rearrange("(p a) -> p a", a=1)).then_inc(consts_in, 16)
            sp.dma_start(rw2[:, :], t["L0_ffn_router_w2"]).then_inc(consts_in, 16)
            sp.dma_start(rb2[:, :], t["L0_ffn_router_b2"].partition_broadcast(P)).then_inc(consts_in, 16)
            for n in range(2):
                for e in range(NE):
                    sp.dma_start(eb[:, n, e, :], t[f"L0_ffn_expert_b{n + 1}"][e, :].rearrange(
                        "(k p) -> p k", p=P)).then_inc(consts_in, 16)
            sp.dma_start(eb3[:, :], t["L0_ffn_expert_b3"]).then_inc(consts_in, 16)
            sp.wait_ge(flag_set, 2)
            sp.dma_start(base_dram.rearrange("(b p) -> p b", p=RP), base_i[0:RP, :]).then_inc(bases_out, 16)
            sp.wait_ge(bases_out, 16)
            sp.dma_start(base_l[:, :], base_dram.rearrange("(a n) -> a n", a=1)).then_inc(bases_in, 16)
            for c in range(NXC):
                last = NB - 1 if c == NXC - 1 else (c + 1) * XC
                sp.wait_ge(normed, last)
                sp.dma_start(h_tab[0][c * XC * P:last * P, :].rearrange("(b q) d -> q b d", q=P),
                             xbig[:, c * XC:last, :]).then_inc(table_out, 16)
            sp.wait_ge(normed, NB)
            sp.dma_start(h_tab[0][(NB - 1) * P:N, :], xbig[0:LAST, NB - 1, :]).then_inc(table_out, 16)
            sp.wait_ge(turned, 2 * RB)
            for n in range(3):
                for e in range(NE):
                    sp.dma_start(we[:, n, e, :, :], t[f"L0_ffn_expert_w{n + 1}"][e, :, :].rearrange(
                        "(k p) h -> p k h", p=P)).then_inc(we_in, 16)
            for u in range(2):
                sp.sem_inc(hb_free[u], 1)
                sp.sem_inc(acc_free[u], 1)

            def store_chunk(i, u):
                row = ahead(sp, i, NXC // 2) * (2 * XC * P) + (1 - u) * (XC * P)
                sp.wait_ge(hb_set, i * (2 * XC) + ((u + 1) * XC + 1))
                alone(sp, "sp")
                sp.dma_start(h_tab[1][bass.ds(row, XC * P), :].rearrange("(b q) d -> q b d", q=P),
                             hb[:, u, :, :]).then_inc(hb_out[u], 16)

            def free_chunk(i, u):
                sp.wait_ge(hb_out[u], i * 16 + 16)
                sp.sem_inc(hb_free[u], 1)

            sp.wait_ge(hb_set, XC + 1)
            sp.dma_start(h_tab[1][(NB - XC) * P:(NB - 1) * P, :].rearrange("(b q) d -> q b d", q=P),
                         hb[:, 0, 0:XC - 1, :]).then_inc(hb_end, 16)
            sp.dma_start(h_tab[1][(NB - 1) * P:N, :], hb[0:LAST, 0, XC - 1, :]).then_inc(hb_out[0], 16)
            sp.wait_ge(hb_end, 16)
            free_chunk(0, 0)
            store_chunk(0, 1)
            if NXC > 2:
                with sp.Fori(1, NXC // 2) as i:
                    store_chunk(i, 0)
                    free_chunk(i - 1, 1)
                    store_chunk(i, 1)
                    free_chunk(i, 0)

            def load_x(q, u, rows_n):
                row = column(ahead(sp, q, HB), u)
                if not isinstance(q, int) or q > 0:
                    sp.wait_ge(xr_set, 2 * q + (u - 1))
                    alone(sp, "sp")
                sp.dma_start(xin[0:rows_n, u, :], t["x"][bass.ds(row, rows_n), :]).then_inc(xin_in[u], 16)

            def store_out(q, u, rows_n):
                row = column(ahead(sp, q, HB), u)
                if not isinstance(q, int) or q > 0:
                    sp.wait_ge(out_st[u], q * 16)
                    sp.sem_inc(acc_free[u], 1)
                sp.wait_ge(h3_ev, (2 * q + (u + 1)) * NE + 3)
                alone(sp, "sp")
                sp.dma_start(out[bass.ds(row, rows_n), :], acc[0:rows_n, u, :]).then_inc(out_st[u], 16)

            load_x(0, 0, LAST)
            load_x(0, 1, P)
            load_x(1, 0, P)
            store_out(0, 0, LAST)
            load_x(1, 1, P)
            store_out(0, 1, P)
            with sp.Fori(1, HB - 1) as i:
                for u in range(2):
                    load_x(i + 1, u, P)
                    store_out(i, u, P)
            store_out(HB - 1, 0, P)
            store_out(HB - 1, 1, P)
            for u in range(2):
                sp.wait_ge(out_st[u], 16 * HB)

        @block.gpsimd
        def _(pool):
            nc.gpsimd.memset(src_i[:, RB - 1, :], int(FAR))
            nc.gpsimd.memset(dst_i[:, RB - 1, :], int(FAR))
            nc.gpsimd.memset(xbig[:, NB - 1, :], 0.0)
            nc.gpsimd.memset(xin[:, 0, :], 0.0)
            pool.drain().then_inc(filled, 1)
            nc.gpsimd.iota(iota_i[:, :], pattern=[[1, P]], base=0, channel_multiplier=0).then_inc(filled, 1)
            nc.gpsimd.iota(gid_i[:, :], pattern=[[RP, RB]], base=0, channel_multiplier=1).then_inc(filled, 1)
            nc.gpsimd.memset(idxT[:, 0:TPI], 0).then_inc(filled, 1)
            nc.gpsimd.iota(iota_p[:, :], pattern=[[0, 1]], base=0, channel_multiplier=1).then_inc(filled, 1)
            nc.gpsimd.memset(ones[:, :], 1.0).then_inc(filled, 1)
            nc.gpsimd.memset(zero_b[:, :], 0.0).then_inc(filled, 1)
            nc.gpsimd.memset(zeros[:, :], 0.0).then_inc(filled, 1)
            pool.wait_ge(table_out, 16 * (NXC + 1))
            nc.gpsimd.memset(aggT[:, KD - 1, :], 0.0).then_inc(agg_zero, 1)
            pool.wait_ge(flag_set, 1)
            flag = nc.gpsimd.value_load(fast_i[0:1, 0:1], min_val=0, max_val=1)

            def gather_group(j, indices, k, tab, got):
                alone(pool, "pool")
                for h in range(TPG):
                    pool.indirect_dma_start(gath[:, j, h, :], None, tab, bass.IndirectOffsetOnAxis(
                        indices[:, k + h:k + h + 1], 0)).then_inc(got, 16)

            def gathers(layer):
                with pool.If(flag):
                    with pool.Fori(0, ITERS) as it:
                        for j in range(GPI):
                            c, k = divmod(j * TPG, CHUNK)
                            if k == 0:
                                pool.wait_ge(idx_set[c], it + (layer * ITERS + 1))
                            pool.wait_ge(agg_mm, it * GPI + (layer * ITERS * GPI + j + 1))
                            gather_group(j, idx[c], k, h_tab[layer], rows_got[j])
                with pool.Else():
                    with pool.Fori(0, NG) as g:
                        pool.wait_ge(gen_idx, g + (layer * NG + 1))
                        gather_group(0, idx[0], 0, h_tab[layer], gen_rows)

            gathers(0)
            with pool.Fori(0, HB) as i:
                left = ahead(pool, i, HB)
                for u in range(2):
                    pool.wait_ge(staged[u], i + 1)
                    nc.gpsimd.tensor_copy(aggT[:, :, bass.ds(column(left, u), P)],
                                          zeros[:, :].rearrange("p (k n) -> p k n", k=KD)).then_inc(cleared[u], 1)
            for u in range(2):
                pool.wait_ge(hb_out[u], 16 * (NXC // 2))
            gathers(1)

        @block.scalar
        def _(act):
            act.sem_inc(h1_set, 2)
            act.sem_inc(h2_set, 2)
            act.wait_ge(flag_set, 1)
            flag = nc.scalar.value_load(fast_i[0:1, 0:1], min_val=0, max_val=1)

            def lay_chunk(layer, it, c):
                col = (ITERS - it) * TPI if isinstance(it, int) else act.snap(it * (-TPI) + ITERS * TPI, min_val=0)
                act.wait_ge(agg_mm, it * GPI + (layer * ITERS * GPI + (c + 1) * (GPI // 2)))
                nc.scalar.copy(idx[c][:, :], idxT[:, bass.ds(col + c * CHUNK, CHUNK)]).then_inc(idx_set[c], 1)

            def lay_general(layer):
                with act.Fori(0, NG) as g:
                    act.wait_ge(gen_mm, g * NW + (layer * NG * NW + 1))
                    nc.scalar.copy(idx[0][:, 0:TPG], idxT[:, bass.ds(g * TPG + TPI, TPG)]).then_inc(gen_idx, 1)

            def stage_block(left, u, uses):
                act.wait_ge(conv_mm[u], uses + 1)
                nc.scalar.copy(stage[:, u, :, :], aggT[:, :, bass.ds(column(left, u), P)]).then_inc(staged[u], 1)

            act.wait_ge(vstep, V_IDX)
            act.wait_ge(consts_in, 16 * N_CONST)
            with act.If(flag):
                with act.Fori(0, ITERS) as it:
                    for c in range(2):
                        lay_chunk(0, it, c)
            with act.Else():
                lay_general(0)
            act.wait_ge(agg_done, 1)
            with act.Fori(0, HB) as i:
                left = ahead(act, i, HB)
                for u in range(2):
                    stage_block(left, u, i)

            def body(q, u, front, experts, it=None):
                m = 2 * q + u

                def rectify(ready, done, used, src, dst, layer, e):
                    src = src.rearrange("p (k n) -> p k n", k=KD)
                    k = (m - 1) * NE + e
                    act.wait_ge(ready, k + 3)
                    act.wait_ge(used, k + 1)
                    for c in range(KD):
                        ins = nc.scalar.activation(dst[:, e % 2, c, :], src[:, c, :], ACT.Relu,
                                                   bias=eb[:, layer, e, c:c + 1])
                    ins.then_inc(done, 1)

                if front:
                    left = ahead(act, q, HB)
                    if it is not None:
                        act.wait_ge(agg_add, it * GPI + (ITERS * GPI + AGG_SLOTS))
                    stage_block(left, u, q + HB)
                if it is not None:
                    lay_chunk(1, it, 1)
                for n, (what, e) in enumerate(expert_order()):
                    if it is not None and n == 15:
                        lay_chunk(1, it + 1, 0)
                    if what == "l1" and experts:
                        rectify(h1_mm, h1_set, h2_mm, exp_bank("l1", e, 1 - u), h1T, 0, e)
                    if what == "l2" and experts:
                        rectify(h2_mm, h2_set, h3_mm, exp_bank("l2", e, 1 - u), h2T, 1, e)
                    if what == "gT" and experts:
                        act.wait_ge(gT_mm, m)
                        act.wait_ge(b3_mm, m)
                        nc.scalar.copy(gateT, p_gT).then_inc(gT_set, 1)
                    if what == "tr" and front:
                        act.wait_ge(xnT_mm, m + 1)
                        nc.scalar.copy(xnT[:, u, :, :], p_xnT).then_inc(xnT_set, 1)
                    if what == "rh" and front:
                        act.wait_ge(rh_mm, m + 1)
                        nc.scalar.activation(rhT[:, :], p_rh, ACT.Relu, bias=rb1[:, 0:1]).then_inc(rh_set, 1)
                    if what == "lg" and front:
                        act.wait_ge(lmax_set, m + 1)
                        nc.scalar.activation(pexp[:, :], lg[:, :], ACT.Exp, bias=lmax[:, 0:1],
                                             accum_out=psumr[:, 0:1]).then_inc(pe_set, 1)
                if front:
                    act.wait_ge(wd_set, m + 1)
                    nc.scalar.activation(w12[:, 1:2], w12[:, 0:1], ACT.Exp).then_inc(wx_set, 1)

            with act.If(flag):
                lay_chunk(1, 0, 0)
                fused(act, body, 2 * ITERS * GPI + AGG_SLOTS)
            with act.Else():
                lay_general(1)
                act.wait_ge(agg_done, 2)
                bodies(act, body)

        @block.tensor
        def _(pe):
            mm = nc.tensor.matmul
            pe.sem_inc(deg_mm, 2)
            pe.sem_inc(agg_mm, GPI)
            pe.sem_inc(gen_mm, 1)
            pe.sem_inc(b3_mm, 1)
            for s in (h1_mm, h2_mm, h3_mm):
                pe.sem_inc(s, 2)
            for u in range(2):
                pe.sem_inc(conv_mm[u], 1)
            pe.wait_ge(filled, N_FILL)
            pe.wait_ge(vstep, V_BAD)
            mm(p_bad, ones[0:RP, 0:RP], bad[0:RP, 1:2], start=True, stop=True).then_inc(bad_sum, 1)
            pe.wait_ge(flag_set, 1)
            flag = nc.tensor.value_load(fast_i[0:1, 0:1], min_val=0, max_val=1)

            def turn_rows(tables, n):
                for rb in range(RB):
                    k = n * RB + rb
                    if k >= 2:
                        pe.wait_ge(unturned, k - 1)
                    for a, table in enumerate(tables):
                        for h in range(TPG):
                            ins = nc.tensor.transpose(p_rows[k % 2][:, a, h, 0:RP], table[0:RP, rb, h * P:(h + 1) * P],
                                                      ident[0:RP, 0:RP])
                    ins.then_inc(turned, 1)

            pe.wait_ge(vstep, V_LOC)
            turn_rows((src_f, loc_f), 0)

            def degree_open(n):
                mm(p_deg[n], zero_b[:, :], zero_b[:, 0:NB], start=True, stop=False, skip_group_check=True)

            def degree_batch(n, it, k):
                b = n * DEG_ALL + k
                pe.wait_ge(deg_oh, it * BPI + (b + 1))
                for i in range(TPB):
                    ins = mm(p_deg[n], hlo[:, k % 2, i, :], hhi[:, k % 2, i, :], start=False, stop=False, skip_group_check=True)
                ins.then_inc(deg_mm, 1)

            def degree_close(n):
                mm(p_deg[n], zero_b[:, :], zero_b[:, 0:NB], start=False, stop=True, skip_group_check=True).then_inc(deg_end, 1)

            def degree_loop(n):
                with pe.Fori(0, ITERS) as it:
                    for k in range(BPI):
                        degree_batch(n, it, k)

            degree_open(0)
            degree_loop(0)
            degree_close(0)
            turn_rows((dst_f,), 1)
            degree_open(1)

            def group_products(psum, j, oh):
                for c in range(KD):
                    for h in range(TPG):
                        ins = mm(psum[:, c, :], gath[:, j, h, c * P:(c + 1) * P], oh[h], start=(h == 0), stop=(h == TPG - 1))
                return ins

            def aggregate_group(layer, it, j):
                k, i = divmod(j * TPG, TPB)
                if i == 0:
                    pe.wait_ge(oh_set, it * BPI + (layer * ITERS * BPI + k + 1))
                pe.wait_ge(agg_add, it * GPI + (layer * ITERS * GPI + j + 1))
                pe.wait_ge(rows_got[j], it * (16 * TPG) + 16 * TPG * (layer * ITERS + 1))
                group_products(p_agg[j % AGG_SLOTS], j, [oneh[:, k, i + h, :] for h in range(TPG)]).then_inc(agg_mm, 1)

            def aggregate_general(layer):
                with pe.Fori(0, NG) as g:
                    pe.wait_ge(gen_rows, g * (16 * TPG) + 16 * TPG * (layer * NG + 1))
                    alone(pe, "pe")
                    with pe.Fori(0, NW) as w:
                        pe.wait_ge(gen_oh, g * NW + w + (layer * NG * NW + 1))
                        group_products(p_agg[0], 0, [oneh[:, 0, h, :] for h in range(TPG)]).then_inc(gen_mm, 1)

            def conv(layer, u, uses, psum):
                pe.wait_ge(staged[u], uses + 1)
                for k in range(KD):
                    ins = mm(psum, stage[:, u, k, :], cw[:, layer, k, :], start=(k == 0), stop=(k == KD - 1))
                ins.then_inc(conv_mm[u], 1)

            with pe.If(flag):
                with pe.Fori(0, ITERS) as it:
                    for j in range(GPI):
                        if j % (TPB // TPG) == 0:
                            degree_batch(1, it, j // (TPB // TPG))
                        aggregate_group(0, it, j)
            with pe.Else():
                degree_loop(1)
                aggregate_general(0)
            degree_close(1)
            pe.wait_ge(consts_in, 16 * N_CONST)
            with pe.Fori(0, HB) as i:
                for u in range(2):
                    pe.wait_ge(conv_ev[u], i + 1)
                    conv(0, u, i, p_conv1[u])
            pe.wait_ge(we_in, 16 * 3 * NE)

            def body(q, u, front, experts, it=None):
                m = 2 * q + u
                v = 1 - u

                def bank_free(what, e):
                    was, e0, back = exp_before(what, e)
                    done, credit = {"l1": (h1_set, 2), "l2": (h2_set, 2), "l3": (h3_ev, 3)}[was]
                    pe.wait_ge(done, (m - 1) * NE + (e0 + 1 + credit - back * NE))

                for n, (what, e) in enumerate(expert_order()):
                    if it is not None and n % 3 == 2:
                        aggregate_group(1, it, n // 3)
                    k = (m - 1) * NE + e
                    if what == "l1" and experts:
                        if e == 0:
                            pe.wait_ge(xnT_set, m)
                        bank_free(what, e)
                        psum = exp_bank(what, e, v).rearrange("p (k n) -> p k n", k=KD)
                        for c in range(KD):
                            for i in range(KD):
                                ins = mm(psum[:, c, :], we[:, 0, e, i, c * P:(c + 1) * P], xnT[:, v, i, :],
                                         start=(i == 0), stop=(i == KD - 1))
                        ins.then_inc(h1_mm, 1)
                    if what == "l2" and experts:
                        pe.wait_ge(h1_set, k + 3)
                        bank_free(what, e)
                        psum = exp_bank(what, e, v).rearrange("p (k n) -> p k n", k=KD)
                        for c in range(KD):
                            for i in range(KD):
                                ins = mm(psum[:, c, :], we[:, 1, e, i, c * P:(c + 1) * P], h1T[:, e % 2, i, :],
                                         start=(i == 0), stop=(i == KD - 1))
                        ins.then_inc(h2_mm, 1)
                    if what == "l3" and experts:
                        pe.wait_ge(h2_set, k + 3)
                        bank_free(what, e)
                        for i in range(KD):
                            ins = mm(exp_bank(what, e, v), h2T[:, e % 2, i, :], we[:, 2, e, i, :], start=(i == 0), stop=(i == KD - 1))
                        ins.then_inc(h3_mm, 1)
                    if what == "gT" and experts:
                        pe.wait_ge(gate_set, m)
                        nc.tensor.transpose(p_gT, gate[:, v, :], ident[:, :]).then_inc(gT_mm, 1)
                    if what == "b3" and experts:
                        pe.wait_ge(gT_set, m)
                        if front:
                            pe.wait_ge(conv_ev[u], q + (HB + 2))
                        else:
                            pe.wait_ge(acc_init, m)
                        mm(p_b3, gateT, eb3[:, :], start=True, stop=True).then_inc(b3_mm, 1)
                    if what == "conv" and front:
                        need(pe, rh_set, m)
                        conv(1, u, q + HB, p_conv)
                    if what == "tr" and front:
                        pe.wait_ge(xn_set, m + 1)
                        need(pe, xnT_set, m)
                        for i in range(KD):
                            ins = nc.tensor.transpose(p_xnT[:, i, :], xn[:, i * P:(i + 1) * P], ident[:, :])
                        ins.then_inc(xnT_mm, 1)
                    if what == "rh" and front:
                        pe.wait_ge(xnT_set, m + 1)
                        if experts:
                            pe.wait_ge(acc_init, m + 1)
                        for i in range(KD):
                            ins = mm(p_rh, rw1[:, i, :], xnT[:, u, i, :], start=(i == 0), stop=(i == KD - 1))
                        ins.then_inc(rh_mm, 1)
                    if what == "lg" and front:
                        pe.wait_ge(rh_set, m + 1)
                        mm(p_lg, rhT[:, :], rw2[:, :], start=True, stop=True).then_inc(lg_mm, 1)

            with pe.If(flag):
                fused(pe, body)
            with pe.Else():
                aggregate_general(1)
                bodies(pe, body)

        @block.vector
        def _(dve):
            ve = nc.vector
            dve.sem_inc(agg_add, AGG_SLOTS)
            dve.sem_inc(gen_add, 1)
            dve.sem_inc(gen_loc, 1)
            dve.sem_inc(hb_set, 1)
            dve.sem_inc(acc_init, 1)
            dve.sem_inc(h3_ev, 3)
            for u in range(2):
                dve.sem_inc(conv_ev[u], 1)
            v = Steps(vstep)

            def step(ins):
                v.inc(ins)
                dve.wait_ge(vstep, v.now())

            dve.wait_ge(filled, N_FILL)
            ve.memset(prob[:, :], -1.0)
            step(ve.tensor_copy(iota[:, :], iota_i[:, :]))
            step(ve.tensor_copy(iota_pf[:, :], iota_p[:, :]))
            step(ve.tensor_scalar(ident[:, :], iota[:, :], iota_pf[:, 0:1], None, ALU.is_equal))
            step(ve.tensor_scalar(iota_hi[:, :], iota[:, 0:NB], float(P), None, ALU.mult))
            dve.wait_ge(rows_in, 16 * N_ROWS)
            step(ve.tensor_copy(src_f[0:RP], src_i[0:RP]))
            step(ve.tensor_copy(dst_f[0:RP], dst_i[0:RP]))
            step(ve.tensor_reduce(base_f[0:RP, :], dst_f[0:RP], X, ALU.min))
            step(ve.tensor_scalar(base_f[0:RP, :], base_f[0:RP, :], float(N - 1), None, ALU.min))

            def relative():
                step(ve.tensor_tensor(loc_f[0:RP], dst_f[0:RP], base_f[0:RP, :].unsqueeze(2).to_broadcast([RP, RB, EPG]),
                                      ALU.subtract))

            relative()
            spans = rows[0:RP, 0, :, :]
            step(ve.scalar_tensor_tensor(spans, loc_f[0:RP], FAR / 2, loc_f[0:RP], ALU.is_lt, ALU.mult))
            step(ve.tensor_reduce(bad[0:RP, 0:1], spans.rearrange("p b e -> p (b e)"), X, ALU.max))
            step(ve.tensor_scalar(bad[0:RP, 1:2], bad[0:RP, 0:1], float(WIN), None, ALU.is_ge))
            step(ve.tensor_scalar(gid_i[0:RP, :], gid_i[0:RP, :], -GPI, 4, ALU.bitwise_and, ALU.logical_shift_left))
            step(ve.tensor_copy(bound[0:RP, :], gid_i[0:RP, :]))
            step(ve.tensor_scalar(reach[0:RP, :], base_f[0:RP, :], float(WIN), float(NB * P), ALU.add, ALU.min))
            step(ve.tensor_tensor(reach[0:RP, :], reach[0:RP, :], bound[0:RP, :], ALU.subtract))
            step(ve.tensor_scalar(reach[0:RP, :], reach[0:RP, :], float(P * (NB - ITERS + LAG)), None, ALU.is_gt))
            step(ve.tensor_reduce(bad[0:RP, 0:1], reach[0:RP, :], X, ALU.max))
            step(ve.tensor_tensor(bad[0:RP, 1:2], bad[0:RP, 1:2], bad[0:RP, 0:1], ALU.add))
            assert v.n == V_BAD
            dve.wait_ge(bad_sum, 1)
            step(ve.tensor_scalar(fast[0:RP, :], p_bad, 0.5, None, ALU.is_lt))
            ve.tensor_copy(fast_i[0:RP, :], fast[0:RP, :]).then_inc(flag_set, 1)
            step(ve.tensor_scalar(base_f[0:RP, :], base_f[0:RP, :], fast[0:RP, 0:1], None, ALU.mult))
            ve.tensor_copy(base_i[0:RP, :], base_f[0:RP, :]).then_inc(flag_set, 1)
            relative()
            assert v.n == V_LOC
            dve.wait_ge(flag_set, 2)
            flag = ve.value_load(fast_i[0:1, 0:1], min_val=0, max_val=1)

            def rsqrt(step, y, x, t):
                step(ve.tensor_scalar(t.bitcast(I32), x.bitcast(I32), 1, None, ALU.logical_shift_right))
                step(ve.tensor_scalar(y.bitcast(I32), t.bitcast(I32), -1.0, float(0x5F3759DF), ALU.mult, ALU.add))
                for _ in range(3):
                    step(ve.tensor_tensor(t, y, y, ALU.mult))
                    step(ve.scalar_tensor_tensor(t, t, -0.5, x, ALU.mult, ALU.mult))
                    step(ve.scalar_tensor_tensor(y, t, 1.5, y, ALU.add, ALU.mult))

            def inverse_root(scale, n):
                step(ve.tensor_scalar(deg[:, :], p_deg[n], 1.0, None, ALU.max))
                rsqrt(step, scale[:, :], deg[:, :], dtmp[:, :])

            def unturn(tables, n):
                for rb in range(RB):
                    k = n * RB + rb
                    dve.wait_ge(turned, k + 1)
                    for a, table in enumerate(tables):
                        ins = ve.tensor_copy(table.rearrange("p (g h) -> p g h", h=TPG)[:, rb * RP:(rb + 1) * RP, :],
                                             p_rows[k % 2][:, a, :, 0:RP].rearrange("p h n -> p n h"))
                    ins.then_inc(unturned, 1)
                dve.wait_ge(unturned, (n + 1) * RB)

            def split_ids():
                lo_i = loT.bitcast(I32)
                step(ve.tensor_copy(lo_i, hiT))
                step(ve.tensor_scalar(lo_i, lo_i, P - 1, None, ALU.bitwise_and))
                step(ve.tensor_copy(loT, lo_i))
                step(ve.tensor_tensor(hiT, hiT, loT, ALU.subtract))

            unturn((hiT, locT[:, :]), 0)
            step(ve.tensor_scalar(idxT[:, TPI:], hiT, float(N - 1), None, ALU.min))
            assert v.n == V_IDX
            split_ids()

            def degree_batch(n, it, k):
                b = n * DEG_ALL + k
                dve.wait_ge(deg_mm, it * BPI + (b + 1))
                t0 = it * TPI + k * TPB
                ve.tensor_tensor(hlo[:, k % 2, :, :], iota[:, :].unsqueeze(1).to_broadcast([P, TPB, P]),
                                 loT[:, bass.ds(t0, TPB)].unsqueeze(2).to_broadcast([P, TPB, P]), ALU.is_equal)
                ve.tensor_tensor(hhi[:, k % 2, :, :], iota_hi[:, :].unsqueeze(1).to_broadcast([P, TPB, NB]),
                                 hiT[:, bass.ds(t0, TPB)].unsqueeze(2).to_broadcast([P, TPB, NB]), ALU.is_equal).then_inc(deg_oh, 1)

            def degree_loop(n):
                with dve.Fori(0, ITERS) as it:
                    for k in range(BPI):
                        degree_batch(n, it, k)

            degree_loop(0)
            dve.wait_ge(deg_end, 1)
            inverse_root(out_s, 0)
            dve.wait_ge(x_in, 16 * (NXC + 1))
            with dve.Fori(0, NXC) as c:
                v.enter(c, XC)
                for i in range(XC):
                    b = c * XC + i
                    v.inc(ve.bn_stats(stat[:, bass.ds(b, 1), :].rearrange("p a s -> p (a s)"),
                                      xbig[:, bass.ds(b, 1), :].rearrange("p a d -> p (a d)")))
            v.leave(NXC)
            dve.wait_ge(vstep, v.now())
            step(ve.tensor_tensor(mean[:, :], stat[:, :, 1], stat[:, :, 4], ALU.add))
            step(ve.tensor_scalar(mean[:, :], mean[:, :], 0.5, None, ALU.mult))
            step(ve.tensor_tensor(mdif[:, :], stat[:, :, 1], mean[:, :], ALU.subtract))
            step(ve.tensor_tensor(mdif[:, :], mdif[:, :], mdif[:, :], ALU.mult))
            step(ve.tensor_tensor(rstd[:, :], stat[:, :, 2], stat[:, :, 5], ALU.add))
            step(ve.scalar_tensor_tensor(rstd[:, :], rstd[:, :], 1.0 / D, mdif[:, :], ALU.mult, ALU.add))
            step(ve.tensor_scalar(mdif[:, :], rstd[:, :], 1e-5, None, ALU.add))
            rsqrt(step, rstd[:, :], mdif[:, :], dtmp[:, :])
            step(ve.tensor_tensor(rstd[:, :], rstd[:, :], out_s[:, :], ALU.mult))
            with dve.Fori(0, NXC) as c:
                for i in range(XC):
                    b = c * XC + i
                    xb = xbig[:, bass.ds(b, 1), :].rearrange("p a d -> p (a d)")
                    ve.tensor_scalar(xb, xb, mean[:, bass.ds(b, 1)], rstd[:, bass.ds(b, 1)],
                                     ALU.subtract, ALU.mult).then_inc(normed, 1)
            unturn((hiT,), 1)
            split_ids()
            dve.wait_ge(table_out, 16 * (NXC + 1))
            ve.memset(aggT[:, 0:KD - 1, :], 0.0).then_inc(agg_zero, 1)
            dve.wait_ge(agg_zero, 2)
            dve.wait_ge(bases_in, 16)

            def add_group(where, psum, done):
                ve.tensor_tensor(aggT[:, :, where], aggT[:, :, where], psum, ALU.add).then_inc(done, 1)

            def one_hot(oh, local, tiles):
                return ve.tensor_tensor(oh, iota[:, 0:WIN].unsqueeze(1).to_broadcast([P, tiles, WIN]),
                                        local.unsqueeze(2).to_broadcast([P, tiles, WIN]), ALU.is_equal)

            def aggregate_batch(layer, it, k):
                col = (ITERS - 1 - it) * TPI if isinstance(it, int) else dve.snap(it * (-TPI) + (ITERS - 1) * TPI, min_val=0)
                dve.wait_ge(agg_mm, it * GPI + (layer * ITERS * GPI + (k + 1) * (TPB // TPG)))
                one_hot(oneh[:, k, :, :], locT[:, bass.ds(col + k * TPB, TPB)], TPB).then_inc(oh_set, 1)

            def aggregate_add(layer, it, j):
                at = (ITERS - 1 - it) * GPI if isinstance(it, int) else dve.snap(it * (-GPI) + (ITERS - 1) * GPI, min_val=0)
                base = ve.value_load(base_l[0:1, bass.ds(at + j, 1)], min_val=0, max_val=N - 1)
                done = it * GPI + (layer * ITERS * GPI + j)
                dve.wait_ge(agg_mm, done + (GPI + 1))
                dve.wait_ge(agg_add, done + AGG_SLOTS)
                add_group(bass.ds(base, WIN), p_agg[j % AGG_SLOTS], agg_add)

            def aggregate_general(layer):
                with dve.Fori(0, NG) as g:
                    n0 = g * NW + layer * NG * NW
                    dve.wait_ge(gen_add, n0 + 1)
                    dve.wait_ge(gen_loc, g * (NW + 1) + (layer * NG * (NW + 1) + 1))
                    ve.tensor_copy(locw[:, :], locT[:, bass.ds(g * TPG, TPG)]).then_inc(gen_loc, 1)
                    with dve.Fori(0, NW) as w:
                        dve.wait_ge(gen_loc, g * (NW + 1) + w + (layer * NG * (NW + 1) + 2))
                        one_hot(oneh[:, 0, 0:TPG, :], locw[:, :], TPG).then_inc(gen_oh, 1)
                        dve.wait_ge(gen_oh, n0 + w + 1)
                        ve.tensor_scalar(locw[:, :], locw[:, :], float(-WIN), None, ALU.add).then_inc(gen_loc, 1)
                        dve.wait_ge(gen_mm, n0 + w + 2)
                        add_group(bass.ds(w * WIN, WIN), p_agg[0], gen_add)
                        dve.wait_ge(gen_add, n0 + w + 2)
                        alone(dve, "dve")
                dve.sem_inc(agg_done, 1)

            with dve.If(flag):
                with dve.Fori(0, ITERS) as it:
                    def batch(k):
                        aggregate_batch(0, it, k)
                        degree_batch(1, it, k)

                    batch(0)
                    for k in range(BPI):
                        if k + 1 < BPI:
                            batch(k + 1)
                        for j in range(k * (TPB // TPG), (k + 1) * (TPB // TPG)):
                            aggregate_add(0, it, j)
                dve.wait_ge(agg_add, ITERS * GPI + AGG_SLOTS)
                dve.sem_inc(agg_done, 1)
            with dve.Else():
                degree_loop(1)
                aggregate_general(0)
            dve.wait_ge(deg_end, 2)
            inverse_root(in_s, 1)
            dve.wait_ge(consts_in, 16 * N_CONST)

            def conv_out(layer, psum, b, u, uses):
                dve.wait_ge(conv_mm[u], uses + 2)
                ve.scalar_tensor_tensor(tb[:, u, :], psum, in_s[:, bass.ds(b, 1)], cb[:, layer, :],
                                        ALU.mult, ALU.add).then_inc(conv_ev[u], 1)
                dve.wait_ge(conv_ev[u], uses + 2)

            with dve.Fori(0, NXC // 2) as i:
                left = ahead(dve, i, NXC // 2)
                for n in range(2 * XC):
                    u, c, at = n % 2, n // XC, 2 * XC - 1 - n
                    dve.wait_ge(hb_set, i * (2 * XC) + max(n, 1))
                    conv_out(0, p_conv1[u], left * (2 * XC) + at, u, i * XC + n // 2)
                    if n % XC == 0:
                        dve.wait_ge(hb_free[c], i + 1)
                    ve.tensor_scalar(hb[:, c, at % XC, :], tb[:, u, :], 0.0,
                                     out_s[:, bass.ds(left * (2 * XC) + at, 1)], ALU.max, ALU.mult).then_inc(hb_set, 1)
            for u in range(2):
                dve.wait_ge(cleared[u], HB)
            s = None

            def bs(ins):
                s.inc(ins)
                dve.wait_ge(bstep, s.now())

            def body(q, u, front, experts, it=None):
                m = 2 * q + u

                def add(j):
                    if it is not None:
                        aggregate_add(1, it, j)

                def batch(k):
                    if it is not None:
                        aggregate_batch(1, it, k)

                batch(0)
                batch(1)
                add(0)
                w = 1 - u
                if front:
                    conv_out(1, p_conv, ahead(dve, q, HB) * 2 + (1 - u), u, q + HB)
                    dve.wait_ge(xin_in[u], q * 16 + 16)
                    ve.scalar_tensor_tensor(xr[:, u, :], tb[:, u, :], 0.0, xin[:, u, :], ALU.max, ALU.add).then_inc(xr_set, 1)
                add(1)
                if front:
                    dve.wait_ge(xr_set, m + 1)
                    bs(ve.bn_stats(st6[:, :], xr[:, u, :]))
                    alone(dve, "dve")
                    bs(ve.bn_aggr(mv[:, :], st6[:, :]))
                    bs(ve.tensor_scalar(rv[:, :], mv[:, 1:2], 1e-5, None, ALU.add))
                    rsqrt(bs, rs[:, :], rv[:, :], rt[:, :])
                    need(dve, xnT_mm, m)
                    ve.tensor_scalar(xn[:, :], xr[:, u, :], mv[:, 0:1], rs[:, 0:1], ALU.subtract, ALU.mult).then_inc(xn_set, 1)
                    dve.wait_ge(xn_set, m + 1)
                if experts:
                    dve.wait_ge(acc_free[w], q + u)
                    dve.wait_ge(b3_mm, m + 1)
                    ve.tensor_tensor(acc[:, w, :], xr[:, w, :], p_b3, ALU.add).then_inc(acc_init, 1)
                    dve.wait_ge(acc_init, m + 1)
                    dve.wait_ge(gate_set, m)

                def add_expert(e):
                    k = (m - 1) * NE + e
                    dve.wait_ge(h3_mm, k + 3)
                    if e:
                        dve.wait_ge(h3_ev, k + 3)
                    ve.scalar_tensor_tensor(acc[:, w, :], exp_bank("l3", e, w), gate[:, w, e:e + 1], acc[:, w, :],
                                            ALU.mult, ALU.add).then_inc(h3_ev, 1)

                batch(2)
                for e in range(NE - 2):
                    add(e + 2)
                    if e == 1:
                        batch(3)
                    if experts:
                        add_expert(e)
                if front:
                    dve.wait_ge(lg_mm, m + 1)
                    bs(ve.tensor_tensor(lg[:, :], p_lg, rb2[:, :], ALU.add))
                    ve.tensor_reduce(lmax[:, :], lg[:, :], X, ALU.max, negate=True).then_inc(lmax_set, 1)
                add(NE)
                if experts:
                    add_expert(NE - 2)
                if front:
                    dve.wait_ge(pe_set, m + 1)
                    bs(ve.reciprocal(psumr[:, :], psumr[:, :]))
                    bs(ve.tensor_scalar(prob[:, 0:NE], pexp[:, :], psumr[:, 0:1], None, ALU.mult))
                    alone(dve, "dve")
                    bs(ve.max(top[:, :], prob[:, :]))
                    ve.tensor_tensor(w12[:, 0:1], top[:, 1:2], top[:, 0:1], ALU.subtract).then_inc(wd_set, 1)
                    bs(ve.max_index(topi[:, :], top[:, :], prob[:, :]))
                    bs(ve.tensor_copy(topf[:, :], topi[:, :]))
                if experts:
                    add_expert(NE - 1)
                if front:
                    dve.wait_ge(wx_set, m + 1)
                    bs(ve.tensor_scalar(w12[:, 2:3], w12[:, 1:2], 1.0, None, ALU.add))
                    bs(ve.reciprocal(w12[:, 3:4], w12[:, 2:3]))
                    bs(ve.tensor_tensor(w12[:, 2:3], w12[:, 1:2], w12[:, 3:4], ALU.mult))
                    bs(ve.tensor_scalar(gt2[:, :], iota[:, 0:NE], topf[:, 1:2], w12[:, 2:3], ALU.is_equal, ALU.mult))
                    bs(ve.tensor_scalar(gate[:, u, :], iota[:, 0:NE], topf[:, 0:1], w12[:, 3:4], ALU.is_equal, ALU.mult))
                    ve.tensor_tensor(gate[:, u, :], gate[:, u, :], gt2[:, :], ALU.add).then_inc(gate_set, 1)
                add(NE + 1)

            PER_FRONT = 3 + 11 + 1 + 5 + 5

            def counted(q, u, front, experts, it=None):
                if not isinstance(q, int) and u == 1:
                    s.enter(q, 2 * PER_FRONT)
                body(q, u, front, experts, it)
                if not isinstance(q, int) and u == 0:
                    s.leave(HB - 1)

            with dve.If(flag):
                s = Steps(bstep)
                fused(dve, counted)
            with dve.Else():
                aggregate_general(1)
                s = Steps(bstep)
                bodies(dve, counted)


_INS = ["x", "src", "dst", "L0_gnn_W1", "L0_gnn_b1", "L0_gnn_W2", "L0_gnn_b2", "L0_ffn_router_w1", "L0_ffn_router_b1",
        "L0_ffn_router_w2", "L0_ffn_router_b2", "L0_ffn_expert_w1", "L0_ffn_expert_b1", "L0_ffn_expert_w2",
        "L0_ffn_expert_b2", "L0_ffn_expert_w3", "L0_ffn_expert_b3"]


def kernel(**inputs):
    import numpy as _np
    import concourse.bacc as _bacc
    from concourse import mybir as _mybir
    from concourse.bass_utils import run_bass_kernel_spmd as _run

    nc = _bacc.Bacc("TRN2", target_bir_lowering=False, num_devices=1)
    arrays, args = {}, {}
    for name in _INS:
        a = _np.ascontiguousarray(inputs[name])
        arrays[f"in_{name}_dram"] = a
        args[name] = nc.dram_tensor(f"in_{name}_dram", a.shape, _mybir.dt.from_np(a.dtype), kind="ExternalInput").ap()
    out = nc.dram_tensor("out_dram", arrays["in_x_dram"].shape, _mybir.dt.float32, kind="ExternalOutput").ap()
    gnn_experts(nc, args, out)
    r = _run(nc, [arrays], core_ids=[0])
    return r.results[0]["out_dram"]
```

```python
from contextlib import ExitStack

import concourse.bass as bass
from concourse import mybir

P = 128
WIN = 64
TPG = 2
EPG = TPG * P
GPI = 8
TPI = GPI * TPG
TPB = 4
BPI = TPI // TPB
CHUNK = TPI // 2
LAG = 1
PARTS = 3
LOC_MAX = 20000
BASES = 4
AGG_SLOTS = 2
FAR = 1.0e6

F32 = mybir.dt.float32
BF16 = mybir.dt.bfloat16
I16 = mybir.dt.int16
I32 = mybir.dt.int32
U32 = mybir.dt.uint32
ALU = mybir.AluOpType
ACT = mybir.ActivationFunctionType
X = mybir.AxisListType.X


V_BAD = 19
V_LOC = 22
V_IDX = 23
V_IDS = 27


class Steps:

    def __init__(self, sem, credit=0):
        self.sem, self.n, self.it, self.per, self.start = sem, credit, None, 0, 0

    def inc(self, ins):
        ins.then_inc(self.sem, 1)
        self.n += 1

    def enter(self, it, per):
        self.it, self.per, self.start = it, per, self.n

    def leave(self, trips):
        assert self.n - self.start == self.per, (self.n - self.start, self.per)
        self.n, self.it = self.start + self.per * trips, None

    def now(self, ahead=0):
        n = self.n + ahead
        return n if self.it is None else self.it * self.per + n


def gnn_experts(nc, t, out):
    N, D = t["x"].shape
    E = t["src"].shape[0]
    NE, _, H = t["L0_ffn_expert_w1"].shape
    RH = t["L0_ffn_router_w1"].shape[1]
    assert D == 2 * P and H == 2 * P and RH == P and NE <= 8
    KD = D // P
    NB = -(-N // P)
    LAST = N - (NB - 1) * P
    ITERS = -(-E // (EPG * GPI))
    NG = ITERS * GPI
    NT = NG * TPG
    FULLG, REST = E // EPG, E % EPG
    RB = -(-NG // P)
    RP = NG // RB
    assert NG % RB == 0 and RP <= P and GPI * 16 == P
    assert ITERS == NB
    NW = -(-N // WIN)
    COLS = N + WIN
    assert N <= LOC_MAX - WIN
    assert COLS >= NB * P and COLS >= NW * WIN and NB % 2 == 0
    XC = 7
    assert NB % (2 * XC) == 0 and 2 * XC <= TPI
    NXC = NB // XC
    XA = XC * 3 // 7

    h_tab = [nc.dram_tensor("table1", (N, D), F32, kind="Internal").ap(),
             nc.dram_tensor("table2", (N, PARTS * D), BF16, kind="Internal").ap()]
    base_dram = nc.dram_tensor("base_list", (NG,), I32, kind="Internal").ap()

    ctx = ExitStack()
    with ctx:
        ctx.enter_context(nc.allow_non_contiguous_dma(reason="small bias columns and group bases"))

        def sb(name, shape, dt=F32):
            return ctx.enter_context(nc.sbuf_tensor(name, shape, dt))

        def sem(name):
            return ctx.enter_context(nc.semaphore(name))

        big = sb("big", [P, max(NB * D, KD * COLS)])
        xbig = big[:, 0:NB * D].rearrange("p (b d) -> p b d", d=D)
        aggT = big[:, 0:KD * COLS].rearrange("p (k n) -> p k n", k=KD)
        WE = 3 * NE * KD * H
        late = sb("late", [P, max(WE, 4 * RB * EPG)])
        rows = late[:, 0:4 * RB * EPG].rearrange("p (a b e) -> p a b e", a=4, e=EPG)
        src_i, dst_i = rows[:, 0, :, :].bitcast(I32), rows[:, 1, :, :].bitcast(I32)
        src_f, dst_f = rows[:, 2, :, :], rows[:, 3, :, :]
        loc_f = rows[:, 1, :, :]
        we = late[:, 0:WE].rearrange("p (l e k h) -> p l e k h", l=3, e=NE, k=KD)
        idxT = sb("idxT", [P, TPI + NT], I16)
        locT = sb("locT", [P, TPI + NT], I16)
        OH = TPB * (P + NB)
        work = sb("work", [P, max(2 * NT + OH, 14 * D)])
        hiT, loT = work[:, 0:NT], work[:, NT:2 * NT]
        onehots = work[:, 2 * NT:2 * NT + OH].bitcast(BF16).rearrange("p (b n) -> p b n", b=2)

        def lo_hi(batches):
            return (batches[:, :, 0:TPB * P].rearrange("p b (t n) -> p b t n", t=TPB),
                    batches[:, :, TPB * P:].rearrange("p b (t n) -> p b t n", t=TPB))

        hlo, hhi = lo_hi(onehots)
        wrows = work[:, 0:14 * D].rearrange("p (a d) -> p a d", d=D)
        xr = wrows[:, 0:2, :]
        acc = wrows[:, 2:4, :]
        xnT = wrows[:, 4:6, :].rearrange("p b (k n) -> p b k n", k=KD)
        h1T = wrows[:, 6:8, :].rearrange("p b (k n) -> p b k n", k=KD)
        h2T = wrows[:, 8:10, :].rearrange("p b (k n) -> p b k n", k=KD)
        xn = wrows[:, 10, :]
        t_exact, t_rest = wrows[:, 0:2, :], wrows[:, 2:2 + XC, :]
        stage = wrows[:, 11:13, :].rearrange("p b (k n) -> p b k n", k=KD)
        gateT = wrows[0:NE, 13, 0:P]
        base_f = sb("base_f", [P, RB])
        gid_i = sb("gid_i", [P, RB], I32)
        bound = sb("bound", [P, RB])
        reach = sb("reach", [P, RB])
        base_i = sb("base_i", [P, RB], I32)
        base_l = sb("base_l", [1, NG], I32)
        bad = sb("bad", [P, 2])
        fast = sb("fast", [P, 1])
        fast_i = sb("fast_i", [P, 1], I32)
        iota_i = work[:, 0:P].bitcast(I32)
        iota_p = sb("iota_p", [P, 1], I32)
        iota_pf = sb("iota_pf", [P, 1])
        iota = sb("iota", [P, P])
        iota_hi = sb("iota_hi", [P, NB])
        ident = sb("ident", [P, P])
        ones = sb("ones", [P, P])
        zero_b = sb("zero_b", [P, P], BF16)
        cw = sb("cw", [P, 2, KD, D])
        cb = sb("cb", [P, 2, D])
        rw1 = sb("rw1", [P, KD, RH])
        rb1 = sb("rb1", [P, 1])
        rw2 = sb("rw2", [P, NE])
        rb2 = sb("rb2", [P, NE])
        eb = sb("eb", [P, 2, NE, KD])
        eb3 = sb("eb3", [NE, D])
        out_s = sb("out_s", [P, NB])
        in_s = sb("in_s", [P, NB])
        dtmp = sb("dtmp", [P, NB])
        mean = sb("mean", [P, NB])
        mdif = sb("mdif", [P, NB])
        deg = mdif
        rstd = sb("rstd", [P, NB])
        idx = [sb(f"idx{n}", [P, CHUNK], I32) for n in range(2)]
        gath = sb("gath", [P, GPI, TPG, PARTS * D // 2])
        gath_parts = gath[:, :, :, :].bitcast(BF16)
        gath_flat = gath[:, :, :, :].rearrange("p g t d -> p (g t d)")
        hb = gath_flat[:, 0:XC * PARTS * D].bitcast(BF16).rearrange(
            "p (b s d) -> p b s d", b=2 * XC, s=PARTS)
        at = XC * D
        squares = gath_flat[:, at:at + 2 * OH].rearrange("p (b n) -> p b n", b=2)
        at += 2 * OH
        onehots_a = gath_flat[:, at:at + OH].bitcast(BF16).rearrange("p (b n) -> p b n", b=2)
        unused = gath_flat[:, 0:XC * D].rearrange("p (b d) -> p b d", d=D)
        oneh_f = sb("oneh", [P, BPI, TPB, WIN])
        oneh_b = oneh_f[:, 0:BPI // 2, :, :].rearrange("p b t w -> p (b t w)").bitcast(BF16).rearrange(
            "p (b t w) -> p b t w", b=BPI, t=TPB)
        oneh = [oneh_f[:, :, :, :], oneh_b]
        locw = sb("locw", [P, TPG])
        tb = sb("tb", [P, 2, D])
        xin = sb("xin", [P, 2, D])
        st6 = sb("st6", [P, 6])
        mv = sb("mv", [P, 2])
        rs, rv, rt = (sb(n, [P, 1]) for n in ("rs", "rv", "rt"))
        rhT = sb("rhT", [P, P])
        lg = sb("lg", [P, NE])
        lmax = sb("lmax", [P, 1])
        pexp = sb("pexp", [P, NE])
        psumr = sb("psumr", [P, 1])
        prob = sb("prob", [P, 8])
        top = sb("top", [P, 8])
        topi = sb("topi", [P, 8], U32)
        topf = sb("topf", [P, 8])
        w12 = sb("w12", [P, 4])
        gate = sb("gate", [P, 2, NE])
        gt2 = sb("gt2", [P, NE])

        def bank(name):
            return ctx.enter_context(nc.psum_tensor(name, [P, 512], F32))

        b_agg = [bank(f"b_agg{n}") for n in range(AGG_SLOTS)]
        b_front = [bank(f"b_front{n}") for n in range(2)]
        b_exp = [bank(f"b_exp{n}") for n in range(4)]
        p_agg = [b[:, 0:KD * WIN].rearrange("p (k w) -> p k w", k=KD) for b in b_agg]
        p_conv1 = [b[:, 0:D] for b in b_front]
        p_conv = b_front[0][:, 0:D]
        p_b3 = b_front[0][:, D:2 * D]
        p_rh = b_front[0][:, 0:P]
        p_gT = b_front[1][0:NE, 0:P]
        p_xnT = b_front[1][:, 0:D].rearrange("p (k n) -> p k n", k=KD)
        p_lg = b_front[1][:, D:D + NE]
        p_exp = [b[:, 0:D] for b in b_exp]
        p_deg = [b[:, 0:NB] for b in b_exp[0:2]]
        p_rows = [b[:, :].rearrange("p (a h n) -> p a h n", a=2, h=TPG) for b in b_front]
        p_bad = b_exp[2][0:RP, 0:1]

        filled = sem("filled")
        rows_in = sem("rows_in")
        consts_in = sem("consts_in")
        x_in = sem("x_in")
        vstep = sem("vstep")
        bad_sum = sem("bad_sum")
        flag_set = sem("flag_set")
        turned = sem("turned")
        unturned = sem("unturned")
        deg_oh = sem("deg_oh")
        deg_mm = sem("deg_mm")
        sq_set = sem("sq_set")
        deg_oh_a = sem("deg_oh_a")
        deg_mm_a = sem("deg_mm_a")
        deg_end = sem("deg_end")
        bases_out = sem("bases_out")
        bases_in = sem("bases_in")
        x_sums = sem("x_sums")
        norm_set = sem("norm_set")
        normed = sem("normed")
        normed_a = sem("normed_a")
        table_out = sem("table_out")
        agg_zero = sem("agg_zero")
        idx_set = [sem(f"idx_set{n}") for n in range(2)]
        rows_got = [sem(f"rows_got{n}") for n in range(GPI)]
        oh_set = sem("oh_set")
        agg_mm = sem("agg_mm")
        agg_add = sem("agg_add")
        gen_idx = sem("gen_idx")
        gen_rows = sem("gen_rows")
        gen_oh = sem("gen_oh")
        gen_mm = sem("gen_mm")
        gen_add = sem("gen_add")
        gen_loc = sem("gen_loc")
        passed = {n: sem(f"passed_{n}") for n in ("pool", "pe", "dve", "sp", "act")}
        agg_done = sem("agg_done")
        staged = [sem(f"staged{n}") for n in range(2)]
        cleared = sem("cleared")
        conv_mm = [sem(f"conv_mm{n}") for n in range(2)]
        conv_ev = [sem(f"conv_ev{n}") for n in range(2)]
        t_set = sem("t_set")
        rest_set = sem("rest_set")
        mid_set = sem("mid_set")
        hb_set = sem("hb_set")
        hb_out = [sem(f"hb_out{n}") for n in range(2)]
        hb_end = sem("hb_end")
        hb_free = [sem(f"hb_free{n}") for n in range(2)]
        we_in = sem("we_in")
        xin_in = [sem(f"xin_in{n}") for n in range(2)]
        bstep = sem("bstep")
        xr_set = sem("xr_set")
        xn_set = sem("xn_set")
        xnT_mm = sem("xnT_mm")
        xnT_set = sem("xnT_set")
        rh_mm = sem("rh_mm")
        rh_set = sem("rh_set")
        lg_mm = sem("lg_mm")
        lmax_set = sem("lmax_set")
        pe_set = sem("pe_set")
        wd_set = sem("wd_set")
        wx_set = sem("wx_set")
        gate_set = sem("gate_set")
        gT_mm = sem("gT_mm")
        gT_set = sem("gT_set")
        b3_mm = sem("b3_mm")
        h1_mm = sem("h1_mm")
        h2_mm = sem("h2_mm")
        h3_mm = sem("h3_mm")
        h1_set = sem("h1_set")
        h2_set = sem("h2_set")
        acc_init = sem("acc_init")
        h3_ev = sem("h3_ev")
        acc_free = [sem(f"acc_free{n}") for n in range(2)]
        out_st = [sem(f"out_st{n}") for n in range(2)]

        block = ctx.enter_context(nc.Block())

        HB = NB // 2
        N_CONST = 2 * 2 + 4 + 2 * NE + 1
        N_ROWS = 2 * ((1 if FULLG // RP else 0) + (1 if FULLG % RP else 0) + (1 if REST else 0))
        N_FILL = 8
        PAIRS = ITERS * 7 // 20
        SOLO = ITERS - 2 * PAIRS
        DBI = BPI - 1
        DEG_ALL = SOLO * BPI + 2 * PAIRS * DBI
        assert DEG_ALL % 2 == 0

        def need(eng, semaphore, value):
            if not isinstance(value, int) or value > 0:
                eng.wait_ge(semaphore, value)

        def alone(eng, name):
            eng.sem_inc(passed[name], 1)

        def column(left, u):
            return left * (2 * P) + (1 - u) * P

        def expert_order():
            return [("l1", 0), ("l1", 1), ("l2", 0), ("gT", 0), ("conv", 0), ("l1", 2), ("l2", 1), ("b3", 0), ("l3", 0),
                    ("l1", 3), ("l2", 2), ("l3", 1), ("tr", 0), ("l1", 4), ("l2", 3), ("l3", 2), ("rh", 0),
                    ("l1", 5), ("l2", 4), ("l3", 3), ("lg", 0), ("l2", 5), ("l3", 4), ("l3", 5)]

        OUTPUTS = [x for x in expert_order() if x[0] in ("l1", "l2", "l3")]

        def exp_bank(what, e, v):
            return p_exp[(OUTPUTS.index((what, e)) + v * 3 * NE) % 4]

        def exp_before(what, e):
            at = OUTPUTS.index((what, e)) - 4
            return (*OUTPUTS[at], 1 if at < 0 else 0)

        def ahead(eng, q, n):
            return n - 1 - q if isinstance(q, int) else eng.snap(q * (-1) + (n - 1), min_val=0, max_val=n - 1)

        def bodies(eng, body):
            body(0, 0, True, False)
            with eng.Fori(0, HB - 1) as i:
                body(i, 1, True, True)
                body(i + 1, 0, True, True)
            body(HB - 1, 1, True, True)
            body(HB, 0, False, True)

        def fused(eng, body, all_added=None):
            body(0, 0, False, False, 0)
            body(0, 0, True, False, 1)
            with eng.Fori(0, HB - 1) as i:
                body(i, 1, True, True, 2 * i + 2)
                body(i + 1, 0, True, True, 2 * i + 3)
            if all_added:
                eng.wait_ge(agg_add, all_added)
            body(HB - 1, 1, True, True)
            body(HB, 0, False, True)

        @block.sync
        def _(sp):
            sp.wait_ge(filled, 1)
            whole, part = FULLG // RP, FULLG % RP
            for name, rt in (("src", src_i), ("dst", dst_i)):
                if whole:
                    sp.dma_start(rt[0:RP, 0:whole, :], t[name][0:whole * RP * EPG].rearrange(
                        "(b p e) -> p b e", p=RP, e=EPG)).then_inc(rows_in, 16)
                if part:
                    sp.dma_start(rt[0:part, whole, :], t[name][whole * RP * EPG:FULLG * EPG].rearrange(
                        "(p e) -> p e", e=EPG)).then_inc(rows_in, 16)
                if REST:
                    sp.dma_start(rt[part:part + 1, whole, 0:REST], t[name][FULLG * EPG:E].rearrange(
                        "(p e) -> p e", p=1)).then_inc(rows_in, 16)
            for c in range(NXC):
                last = NB - 1 if c == NXC - 1 else (c + 1) * XC
                sp.dma_start(xbig[:, c * XC:last, :], t["x"][c * XC * P:last * P, :].rearrange(
                    "(b q) d -> q b d", q=P)).then_inc(x_in, 16)
            sp.dma_start(xbig[0:LAST, NB - 1, :], t["x"][(NB - 1) * P:N, :]).then_inc(x_in, 16)
            for n in range(2):
                sp.dma_start(cw[:, n, :, :], t[f"L0_gnn_W{n + 1}"].rearrange("(k p) d -> p k d", p=P)).then_inc(consts_in, 16)
                sp.dma_start(cb[:, n, :], t[f"L0_gnn_b{n + 1}"].partition_broadcast(P)).then_inc(consts_in, 16)
            sp.dma_start(rw1[:, :, :], t["L0_ffn_router_w1"].rearrange("(k p) h -> p k h", p=P)).then_inc(consts_in, 16)
            sp.dma_start(rb1[:, :], t["L0_ffn_router_b1"].rearrange("(p a) -> p a", a=1)).then_inc(consts_in, 16)
            sp.dma_start(rw2[:, :], t["L0_ffn_router_w2"]).then_inc(consts_in, 16)
            sp.dma_start(rb2[:, :], t["L0_ffn_router_b2"].partition_broadcast(P)).then_inc(consts_in, 16)
            for n in range(2):
                for e in range(NE):
                    sp.dma_start(eb[:, n, e, :], t[f"L0_ffn_expert_b{n + 1}"][e, :].rearrange(
                        "(k p) -> p k", p=P)).then_inc(consts_in, 16)
            sp.dma_start(eb3[:, :], t["L0_ffn_expert_b3"]).then_inc(consts_in, 16)
            sp.wait_ge(flag_set, 2)
            sp.dma_start(base_dram.rearrange("(b p) -> p b", p=RP), base_i[0:RP, :]).then_inc(bases_out, 16)
            sp.wait_ge(bases_out, 16)
            sp.dma_start(base_l[:, :], base_dram.rearrange("(a n) -> a n", a=1)).then_inc(bases_in, 16)
            for c in range(NXC):
                last = NB - 1 if c == NXC - 1 else (c + 1) * XC
                sp.wait_ge(normed, (c + 1) * (XC - XA))
                sp.wait_ge(normed_a, (c + 1) * XA)
                sp.dma_start(h_tab[0][c * XC * P:last * P, :].rearrange("(b q) d -> q b d", q=P),
                             xbig[:, c * XC:last, :]).then_inc(table_out, 16)
            sp.dma_start(h_tab[0][(NB - 1) * P:N, :], xbig[0:LAST, NB - 1, :]).then_inc(table_out, 16)
            sp.wait_ge(turned, 2 * RB)
            for n in range(3):
                for e in range(NE):
                    sp.dma_start(we[:, n, e, :, :], t[f"L0_ffn_expert_w{n + 1}"][e, :, :].rearrange(
                        "(k p) h -> p k h", p=P)).then_inc(we_in, 16)
            for u in range(2):
                sp.sem_inc(hb_free[u], 1)
                sp.sem_inc(acc_free[u], 1)

            def store_chunk(i, u):
                row = ahead(sp, i, NXC // 2) * (2 * XC * P) + (1 - u) * (XC * P)
                sp.wait_ge(hb_set, i * (2 * XC) + (u + 1) * XC)
                alone(sp, "sp")
                sp.dma_start(h_tab[1][bass.ds(row, XC * P), :].rearrange("(b q) d -> q b d", q=P),
                             hb[:, (1 - u) * XC:(2 - u) * XC, :, :].rearrange("p b s d -> p b (s d)")).then_inc(hb_out[u], 16)

            def free_chunk(i, u):
                sp.wait_ge(hb_out[u], i * 16 + 16)
                sp.sem_inc(hb_free[u], 1)

            sp.wait_ge(hb_set, XC)
            sp.dma_start(h_tab[1][(NB - XC) * P:(NB - 1) * P, :].rearrange("(b q) d -> q b d", q=P),
                         hb[:, XC:2 * XC - 1, :, :].rearrange("p b s d -> p b (s d)")).then_inc(hb_end, 16)
            sp.dma_start(h_tab[1][(NB - 1) * P:N, :], hb[0:LAST, 2 * XC - 1, :, :].rearrange("p s d -> p (s d)")).then_inc(hb_out[0], 16)
            sp.wait_ge(hb_end, 16)
            free_chunk(0, 0)
            store_chunk(0, 1)
            free_chunk(0, 1)
            with sp.Fori(1, NXC // 2) as i:
                for u in range(2):
                    store_chunk(i, u)
                    free_chunk(i, u)

            def load_x(q, u, rows_n):
                row = column(ahead(sp, q, HB), u)
                if not isinstance(q, int) or q > 0:
                    sp.wait_ge(xr_set, 2 * q + (u - 1))
                    alone(sp, "sp")
                sp.dma_start(xin[0:rows_n, u, :], t["x"][bass.ds(row, rows_n), :]).then_inc(xin_in[u], 16)

            def store_out(q, u, rows_n):
                row = column(ahead(sp, q, HB), u)
                if not isinstance(q, int) or q > 0:
                    sp.wait_ge(out_st[u], q * 16)
                    sp.sem_inc(acc_free[u], 1)
                sp.wait_ge(h3_ev, (2 * q + (u + 1)) * NE + 3)
                alone(sp, "sp")
                sp.dma_start(out[bass.ds(row, rows_n), :], acc[0:rows_n, u, :]).then_inc(out_st[u], 16)

            load_x(0, 0, LAST)
            load_x(0, 1, P)
            load_x(1, 0, P)
            store_out(0, 0, LAST)
            load_x(1, 1, P)
            store_out(0, 1, P)
            with sp.Fori(1, HB - 1) as i:
                for u in range(2):
                    load_x(i + 1, u, P)
                    store_out(i, u, P)
            store_out(HB - 1, 0, P)
            store_out(HB - 1, 1, P)
            for u in range(2):
                sp.wait_ge(out_st[u], 16 * HB)

        @block.gpsimd
        def _(pool):
            nc.gpsimd.memset(src_i[:, RB - 1, :], int(FAR))
            nc.gpsimd.memset(dst_i[:, RB - 1, :], int(FAR))
            nc.gpsimd.memset(xbig[:, NB - 1, :], 0.0)
            nc.gpsimd.memset(xin[:, 0, :], 0.0)
            pool.drain().then_inc(filled, 1)
            nc.gpsimd.iota(iota_i[:, :], pattern=[[1, P]], base=0, channel_multiplier=0).then_inc(filled, 1)
            nc.gpsimd.iota(gid_i[:, :], pattern=[[RP, RB]], base=0, channel_multiplier=1).then_inc(filled, 1)
            nc.gpsimd.memset(idxT[:, 0:TPI], 0).then_inc(filled, 1)
            nc.gpsimd.memset(locT[:, 0:TPI], 0.0).then_inc(filled, 1)
            nc.gpsimd.iota(iota_p[:, :], pattern=[[0, 1]], base=0, channel_multiplier=1).then_inc(filled, 1)
            nc.gpsimd.memset(ones[:, :], 1.0).then_inc(filled, 1)
            nc.gpsimd.memset(zero_b[:, :], 0.0).then_inc(filled, 1)
            pool.wait_ge(table_out, 16 * (NXC + 1))
            pool.wait_ge(flag_set, 1)
            flag = nc.gpsimd.value_load(fast_i[0:1, 0:1], min_val=0, max_val=1)

            def gather_group(layer, j, indices, k, got):
                alone(pool, "pool")
                for h in range(TPG):
                    to = gath[:, j, h, 0:D] if layer == 0 else gath_parts[:, j, h, :]
                    pool.indirect_dma_start(to, None, h_tab[layer], bass.IndirectOffsetOnAxis(
                        indices[:, k + h:k + h + 1], 0)).then_inc(got, 16)

            def gathers(layer):
                with pool.If(flag):
                    with pool.Fori(0, ITERS) as it:
                        for j in range(GPI):
                            c, k = divmod(j * TPG, CHUNK)
                            if k == 0:
                                pool.wait_ge(idx_set[c], it + (layer * ITERS + 1))
                            pool.wait_ge(agg_mm, it * GPI + (layer * ITERS * GPI + j + 1))
                            gather_group(layer, j, idx[c], k, rows_got[j])
                with pool.Else():
                    with pool.Fori(0, NG) as g:
                        pool.wait_ge(gen_idx, g + (layer * NG + 1))
                        gather_group(layer, 0, idx[0], 0, gen_rows)

            gathers(0)
            for i in range(NXC // 2):
                for c in range(2):
                    with pool.Fori(0, XC) as j:
                        pool.wait_ge(mid_set, j + ((2 * i + c) * XC + 1))
                        alone(pool, "pool")
                        at = j * (-1) + ((2 - c) * XC - 1)
                        nc.gpsimd.tensor_tensor(hb[:, bass.ds(at, 1), 2, :].rearrange("p b d -> p (b d)"),
                                                t_rest[:, bass.ds(j, 1), :].rearrange("p b d -> p (b d)"),
                                                hb[:, bass.ds(at, 1), 1, :].rearrange("p b d -> p (b d)"),
                                                ALU.subtract).then_inc(hb_set, 1)
                first = (NXC // 2 - 1 - i) * 2 * XC * P
                for u in range(2):
                    pool.wait_ge(staged[u], (i + 1) * XC)
                nc.gpsimd.memset(aggT[:, :, first:first + 2 * XC * P if i else COLS], 0.0).then_inc(cleared, 1)
            for u in range(2):
                pool.wait_ge(hb_out[u], 16 * (NXC // 2))
            gathers(1)

        @block.scalar
        def _(act):
            act.sem_inc(h1_set, 2)
            act.sem_inc(h2_set, 2)
            act.sem_inc(x_sums, 1)

            def block_of_x(b):
                return xbig[:, bass.ds(b, 1), :].rearrange("p a d -> p (a d)")

            act.wait_ge(x_in, 16 * (NXC + 1))
            with act.Fori(0, NXC) as c:
                act.wait_ge(x_sums, c * XC + 1)
                alone(act, "act")
                for i in range(XC):
                    nc.scalar.activation(unused[:, i, :], block_of_x(c * XC + i), ACT.Copy, scale=-1.0 / D,
                                         accum_out=mean[:, bass.ds(c * XC + i, 1)]).then_inc(x_sums, 1)
            with act.Fori(0, NXC) as c:
                act.wait_ge(x_sums, c * XC + (NB + 1))
                alone(act, "act")
                for i in range(XC):
                    nc.scalar.activation(unused[:, i, :], block_of_x(c * XC + i), ACT.Square,
                                         bias=mean[:, bass.ds(c * XC + i, 1)],
                                         accum_out=mdif[:, bass.ds(c * XC + i, 1)]).then_inc(x_sums, 1)
            act.wait_ge(filled, N_FILL)
            act.wait_ge(vstep, V_IDS)
            sq_lo, sq_hi = lo_hi(squares)
            with act.Fori(0, PAIRS) as i:
                for u in range(2):
                    act.wait_ge(deg_mm_a, i * 2 + (u + 1))
                    alone(act, "act")
                    t0 = i * (2 * TPI) + ((SOLO + u) * TPI + DBI * TPB)
                    for n in range(TPB):
                        nc.scalar.activation(sq_lo[:, u, n, :], iota[:, :], ACT.Square, scale=-1.0, bias=loT[:, bass.ds(t0 + n, 1)])
                        ins = nc.scalar.activation(sq_hi[:, u, n, :], iota_hi[:, :], ACT.Square, scale=-1.0,
                                                   bias=hiT[:, bass.ds(t0 + n, 1)])
                    ins.then_inc(sq_set, 1)
                    act.wait_ge(sq_set, i * 2 + (u + 1))
                    nc.scalar.activation(onehots_a[:, u, :], squares[:, u, :], ACT.Relu, scale=-1.0,
                                         bias=ones[:, 0:1]).then_inc(deg_oh_a, 1)
            act.wait_ge(norm_set, 1)
            with act.Fori(0, NXC) as c:
                for i in range(XC - XA, XC):
                    nc.scalar.activation(block_of_x(c * XC + i), block_of_x(c * XC + i), ACT.Identity,
                                         bias=mdif[:, bass.ds(c * XC + i, 1)],
                                         scale=rstd[:, bass.ds(c * XC + i, 1)]).then_inc(normed_a, 1)
            act.wait_ge(flag_set, 1)
            flag = nc.scalar.value_load(fast_i[0:1, 0:1], min_val=0, max_val=1)

            def lay_chunk(layer, it, c):
                col = (ITERS - it) * TPI if isinstance(it, int) else act.snap(it * (-TPI) + ITERS * TPI, min_val=0)
                act.wait_ge(agg_mm, it * GPI + (layer * ITERS * GPI + (c + 1) * (GPI // 2)))
                nc.scalar.copy(idx[c][:, :], idxT[:, bass.ds(col + c * CHUNK, CHUNK)]).then_inc(idx_set[c], 1)

            def lay_general(layer):
                with act.Fori(0, NG) as g:
                    act.wait_ge(gen_mm, g * NW + (layer * NG * NW + 1))
                    nc.scalar.copy(idx[0][:, 0:TPG], idxT[:, bass.ds(g * TPG + TPI, TPG)]).then_inc(gen_idx, 1)

            def stage_block(left, u, uses):
                act.wait_ge(conv_mm[u], uses + 1)
                nc.scalar.copy(stage[:, u, :, :], aggT[:, :, bass.ds(column(left, u), P)]).then_inc(staged[u], 1)

            act.wait_ge(vstep, V_IDX)
            act.wait_ge(consts_in, 16 * N_CONST)

            def clear_half():
                act.wait_ge(table_out, 16 * (NXC + 1))
                nc.scalar.copy(aggT[:, KD - 1, :], zero_b[:, 0:1].to_broadcast([P, COLS])).then_inc(agg_zero, 1)

            with act.If(flag):
                for c in range(2):
                    lay_chunk(0, 0, c)
                clear_half()
                with act.Fori(1, ITERS) as it:
                    for c in range(2):
                        lay_chunk(0, it, c)
            with act.Else():
                clear_half()
                lay_general(0)
            act.wait_ge(agg_done, 1)

            def conv_steps(i, first, last):
                left = ahead(act, i, NXC // 2)

                def stage_next(n):
                    row = left * (2 * XC * P) + (2 * XC - 1 - n) * P
                    act.wait_ge(conv_mm[n % 2], i * XC + (n // 2 + 1))
                    nc.scalar.copy(stage[:, n % 2, :, :], aggT[:, :, bass.ds(row, P)]).then_inc(staged[n % 2], 1)

                if first:
                    stage_next(0)
                    stage_next(1)
                for n in range(2 * XC):
                    u, c, at = n % 2, n // XC, 2 * XC - 1 - n
                    if n < 2 * XC - 2 or not last:
                        stage_next(n + 2)
                    act.wait_ge(conv_ev[u], i * XC + (n // 2 + 2))
                    if n % XC == 0:
                        act.wait_ge(hb_free[c], i + 1)
                        alone(act, "act")
                    scale = out_s[:, bass.ds(left * (2 * XC) + at, 1)]
                    nc.scalar.activation(t_exact[:, u, :], tb[:, u, :], ACT.Relu, scale=scale)
                    nc.scalar.activation(hb[:, at, 0, :], tb[:, u, :], ACT.Relu, scale=scale).then_inc(t_set, 1)

            conv_steps(0, True, False)
            with act.Fori(1, NXC // 2 - 1) as i:
                conv_steps(i, False, False)
            conv_steps(NXC // 2 - 1, False, True)

            def body(q, u, front, experts, it=None):
                m = 2 * q + u

                def rectify(ready, done, used, src, dst, layer, e):
                    src = src.rearrange("p (k n) -> p k n", k=KD)
                    k = (m - 1) * NE + e
                    act.wait_ge(ready, k + 3)
                    act.wait_ge(used, k + 1)
                    for c in range(KD):
                        ins = nc.scalar.activation(dst[:, e % 2, c, :], src[:, c, :], ACT.Relu,
                                                   bias=eb[:, layer, e, c:c + 1])
                    ins.then_inc(done, 1)

                def stage_front():
                    left = ahead(act, q, HB)
                    if it is not None:
                        act.wait_ge(agg_add, it * GPI + (ITERS * GPI + AGG_SLOTS))
                    stage_block(left, u, q + HB)

                if it is not None:
                    lay_chunk(1, it, 1)
                for n, (what, e) in enumerate(expert_order()):
                    if (what, e) == ("l2", 0) and front:
                        stage_front()
                    if it is not None and n == 13:
                        lay_chunk(1, it + 1, 0)
                    if what == "l1" and experts:
                        rectify(h1_mm, h1_set, h2_mm, exp_bank("l1", e, 1 - u), h1T, 0, e)
                    if what == "l2" and experts:
                        rectify(h2_mm, h2_set, h3_mm, exp_bank("l2", e, 1 - u), h2T, 1, e)
                    if what == "gT" and experts:
                        act.wait_ge(gT_mm, m)
                        act.wait_ge(b3_mm, m)
                        nc.scalar.copy(gateT, p_gT).then_inc(gT_set, 1)
                    if what == "tr" and front:
                        act.wait_ge(xnT_mm, m + 1)
                        nc.scalar.copy(xnT[:, u, :, :], p_xnT).then_inc(xnT_set, 1)
                    if what == "rh" and front:
                        act.wait_ge(rh_mm, m + 1)
                        nc.scalar.activation(rhT[:, :], p_rh, ACT.Relu, bias=rb1[:, 0:1]).then_inc(rh_set, 1)
                    if what == "lg" and front:
                        act.wait_ge(lmax_set, m + 1)
                        nc.scalar.activation(pexp[:, :], lg[:, :], ACT.Exp, bias=lmax[:, 0:1],
                                             accum_out=psumr[:, 0:1]).then_inc(pe_set, 1)
                if front:
                    act.wait_ge(wd_set, m + 1)
                    nc.scalar.activation(w12[:, 1:2], w12[:, 0:1], ACT.Exp).then_inc(wx_set, 1)

            with act.If(flag):
                lay_chunk(1, 0, 0)
                fused(act, body, 2 * ITERS * GPI + AGG_SLOTS)
            with act.Else():
                lay_general(1)
                act.wait_ge(agg_done, 2)
                bodies(act, body)

        @block.tensor
        def _(pe):
            mm = nc.tensor.matmul
            pe.sem_inc(deg_mm, 2)
            pe.sem_inc(deg_mm_a, 2)
            pe.sem_inc(agg_mm, GPI)
            pe.sem_inc(gen_mm, 1)
            pe.sem_inc(b3_mm, 1)
            for s in (h1_mm, h2_mm, h3_mm):
                pe.sem_inc(s, 2)
            for u in range(2):
                pe.sem_inc(conv_mm[u], 1)
            pe.wait_ge(filled, N_FILL)
            pe.wait_ge(vstep, V_BAD)
            mm(p_bad, ones[0:RP, 0:RP], bad[0:RP, 1:2], start=True, stop=True).then_inc(bad_sum, 1)
            pe.wait_ge(flag_set, 1)
            flag = nc.tensor.value_load(fast_i[0:1, 0:1], min_val=0, max_val=1)

            def turn_rows(tables, n):
                for rb in range(RB):
                    k = n * RB + rb
                    if k >= 2:
                        pe.wait_ge(unturned, k - 1)
                    for a, table in enumerate(tables):
                        for h in range(TPG):
                            ins = nc.tensor.transpose(p_rows[k % 2][:, a, h, 0:RP], table[0:RP, rb, h * P:(h + 1) * P],
                                                      ident[0:RP, 0:RP])
                    ins.then_inc(turned, 1)

            pe.wait_ge(vstep, V_LOC)
            turn_rows((src_f, loc_f), 0)

            def degree_open(n):
                mm(p_deg[n], zero_b[:, :], zero_b[:, 0:NB], start=True, stop=False, skip_group_check=True)

            def degree_products(n, lo, hi):
                for i in range(TPB):
                    ins = mm(p_deg[n], lo[:, i, :], hi[:, i, :], start=False, stop=False, skip_group_check=True)
                return ins

            def degree_batch(n, before, buf):
                pe.wait_ge(deg_oh, before + 1)
                degree_products(n, hlo[:, buf, :, :], hhi[:, buf, :, :]).then_inc(deg_mm, 1)

            def degree_close(n):
                mm(p_deg[n], zero_b[:, :], zero_b[:, 0:NB], start=False, stop=True, skip_group_check=True).then_inc(deg_end, 1)

            degree_open(0)
            with pe.Fori(0, SOLO) as it:
                for k in range(BPI):
                    degree_batch(0, it * BPI + k, k % 2)
            alo, ahi = lo_hi(onehots_a)
            with pe.Fori(0, PAIRS) as i:
                for u in range(2):
                    for k in range(u * DBI, (u + 1) * DBI):
                        degree_batch(0, i * (2 * DBI) + (SOLO * BPI + k), k % 2)
                    pe.wait_ge(deg_oh_a, i * 2 + (u + 1))
                    degree_products(0, alo[:, u, :, :], ahi[:, u, :, :]).then_inc(deg_mm_a, 1)
            degree_close(0)
            turn_rows((dst_f,), 1)
            degree_open(1)

            def group_products(layer, psum, j, oh):
                parts = [gath[:, j, :, 0:D]] if layer == 0 else [
                    gath_parts[:, j, :, n * D:(n + 1) * D] for n in reversed(range(PARTS))]
                for c in range(KD):
                    terms = [(h, part) for part in parts for h in range(TPG)]
                    for n, (h, part) in enumerate(terms):
                        ins = mm(psum[:, c, :], part[:, h, c * P:(c + 1) * P], oh[h], start=(n == 0), stop=(n == len(terms) - 1))
                return ins

            def aggregate_group(layer, it, j):
                k, i = divmod(j * TPG, TPB)
                if i == 0:
                    pe.wait_ge(oh_set, it * BPI + (layer * ITERS * BPI + k + 1))
                pe.wait_ge(agg_add, it * GPI + (layer * ITERS * GPI + j + 1))
                pe.wait_ge(rows_got[j], it * (16 * TPG) + 16 * TPG * (layer * ITERS + 1))
                group_products(layer, p_agg[j % AGG_SLOTS], j, [oneh[layer][:, k, i + h, :] for h in range(TPG)]).then_inc(agg_mm, 1)

            def aggregate_general(layer):
                with pe.Fori(0, NG) as g:
                    pe.wait_ge(gen_rows, g * (16 * TPG) + 16 * TPG * (layer * NG + 1))
                    alone(pe, "pe")
                    with pe.Fori(0, NW) as w:
                        pe.wait_ge(gen_oh, g * NW + w + (layer * NG * NW + 1))
                        group_products(layer, p_agg[0], 0, [oneh[layer][:, 0, h, :] for h in range(TPG)]).then_inc(gen_mm, 1)

            def conv(layer, u, uses, psum):
                pe.wait_ge(staged[u], uses + 1)
                for k in range(KD):
                    ins = mm(psum, stage[:, u, k, :], cw[:, layer, k, :], start=(k == 0), stop=(k == KD - 1))
                ins.then_inc(conv_mm[u], 1)

            with pe.If(flag):
                with pe.Fori(0, ITERS) as it:
                    for j in range(GPI):
                        if j % (TPB // TPG) == 0:
                            degree_batch(1, it * BPI + (DEG_ALL + j // (TPB // TPG)), j // (TPB // TPG) % 2)
                        aggregate_group(0, it, j)
            with pe.Else():
                with pe.Fori(0, ITERS) as it:
                    for k in range(BPI):
                        degree_batch(1, it * BPI + (DEG_ALL + k), k % 2)
                aggregate_general(0)
            degree_close(1)
            pe.wait_ge(consts_in, 16 * N_CONST)
            with pe.Fori(0, HB) as i:
                for u in range(2):
                    pe.wait_ge(conv_ev[u], i + 1)
                    conv(0, u, i, p_conv1[u])
            pe.wait_ge(we_in, 16 * 3 * NE)

            def body(q, u, front, experts, it=None):
                m = 2 * q + u
                v = 1 - u

                def bank_free(what, e):
                    was, e0, back = exp_before(what, e)
                    done, credit = {"l1": (h1_set, 2), "l2": (h2_set, 2), "l3": (h3_ev, 3)}[was]
                    pe.wait_ge(done, (m - 1) * NE + (e0 + 1 + credit - back * NE))

                for n, (what, e) in enumerate(expert_order()):
                    if it is not None and n % 3 == 1:
                        aggregate_group(1, it, n // 3)
                    k = (m - 1) * NE + e
                    if what == "l1" and experts:
                        if e == 0:
                            pe.wait_ge(xnT_set, m)
                        bank_free(what, e)
                        psum = exp_bank(what, e, v).rearrange("p (k n) -> p k n", k=KD)
                        for c in range(KD):
                            for i in range(KD):
                                ins = mm(psum[:, c, :], we[:, 0, e, i, c * P:(c + 1) * P], xnT[:, v, i, :],
                                         start=(i == 0), stop=(i == KD - 1))
                        ins.then_inc(h1_mm, 1)
                    if what == "l2" and experts:
                        pe.wait_ge(h1_set, k + 3)
                        bank_free(what, e)
                        psum = exp_bank(what, e, v).rearrange("p (k n) -> p k n", k=KD)
                        for c in range(KD):
                            for i in range(KD):
                                ins = mm(psum[:, c, :], we[:, 1, e, i, c * P:(c + 1) * P], h1T[:, e % 2, i, :],
                                         start=(i == 0), stop=(i == KD - 1))
                        ins.then_inc(h2_mm, 1)
                    if what == "l3" and experts:
                        pe.wait_ge(h2_set, k + 3)
                        bank_free(what, e)
                        for i in range(KD):
                            ins = mm(exp_bank(what, e, v), h2T[:, e % 2, i, :], we[:, 2, e, i, :], start=(i == 0), stop=(i == KD - 1))
                        ins.then_inc(h3_mm, 1)
                    if what == "gT" and experts:
                        pe.wait_ge(gate_set, m)
                        nc.tensor.transpose(p_gT, gate[:, v, :], ident[:, :]).then_inc(gT_mm, 1)
                    if what == "b3" and experts:
                        pe.wait_ge(gT_set, m)
                        if front:
                            pe.wait_ge(conv_ev[u], q + (HB + 2))
                        else:
                            pe.wait_ge(acc_init, m)
                        mm(p_b3, gateT, eb3[:, :], start=True, stop=True).then_inc(b3_mm, 1)
                    if what == "conv" and front:
                        need(pe, rh_set, m)
                        conv(1, u, q + HB, p_conv)
                    if what == "tr" and front:
                        pe.wait_ge(xn_set, m + 1)
                        need(pe, xnT_set, m)
                        for i in range(KD):
                            ins = nc.tensor.transpose(p_xnT[:, i, :], xn[:, i * P:(i + 1) * P], ident[:, :])
                        ins.then_inc(xnT_mm, 1)
                    if what == "rh" and front:
                        pe.wait_ge(xnT_set, m + 1)
                        if experts:
                            pe.wait_ge(acc_init, m + 1)
                        for i in range(KD):
                            ins = mm(p_rh, rw1[:, i, :], xnT[:, u, i, :], start=(i == 0), stop=(i == KD - 1))
                        ins.then_inc(rh_mm, 1)
                    if what == "lg" and front:
                        pe.wait_ge(rh_set, m + 1)
                        mm(p_lg, rhT[:, :], rw2[:, :], start=True, stop=True).then_inc(lg_mm, 1)

            with pe.If(flag):
                fused(pe, body)
            with pe.Else():
                aggregate_general(1)
                bodies(pe, body)

        @block.vector
        def _(dve):
            ve = nc.vector
            dve.sem_inc(agg_add, AGG_SLOTS)
            dve.sem_inc(gen_add, 1)
            dve.sem_inc(gen_loc, 1)
            dve.sem_inc(acc_init, 1)
            dve.sem_inc(h3_ev, 3)
            for u in range(2):
                dve.sem_inc(conv_ev[u], 1)
            v = Steps(vstep)

            def step(ins):
                v.inc(ins)
                dve.wait_ge(vstep, v.now())

            dve.wait_ge(filled, N_FILL)
            ve.memset(prob[:, :], -1.0)
            step(ve.tensor_copy(iota[:, :], iota_i[:, :]))
            step(ve.tensor_copy(iota_pf[:, :], iota_p[:, :]))
            step(ve.tensor_scalar(ident[:, :], iota[:, :], iota_pf[:, 0:1], None, ALU.is_equal))
            step(ve.tensor_scalar(iota_hi[:, :], iota[:, 0:NB], float(P), None, ALU.mult))
            dve.wait_ge(rows_in, 16 * N_ROWS)
            step(ve.tensor_copy(src_f[0:RP], src_i[0:RP]))
            step(ve.tensor_copy(dst_f[0:RP], dst_i[0:RP]))
            step(ve.tensor_reduce(base_f[0:RP, :], dst_f[0:RP], X, ALU.min))
            step(ve.tensor_scalar(base_f[0:RP, :], base_f[0:RP, :], float(N - 1), None, ALU.min))

            def relative():
                step(ve.tensor_tensor(loc_f[0:RP], dst_f[0:RP], base_f[0:RP, :].unsqueeze(2).to_broadcast([RP, RB, EPG]),
                                      ALU.subtract))

            relative()
            spans = rows[0:RP, 0, :, :]
            step(ve.scalar_tensor_tensor(spans, loc_f[0:RP], FAR / 2, loc_f[0:RP], ALU.is_lt, ALU.mult))
            step(ve.tensor_reduce(bad[0:RP, 0:1], spans.rearrange("p b e -> p (b e)"), X, ALU.max))
            step(ve.tensor_scalar(bad[0:RP, 1:2], bad[0:RP, 0:1], float(WIN), None, ALU.is_ge))
            step(ve.tensor_scalar(gid_i[0:RP, :], gid_i[0:RP, :], -GPI, 4, ALU.bitwise_and, ALU.logical_shift_left))
            step(ve.tensor_copy(bound[0:RP, :], gid_i[0:RP, :]))
            step(ve.tensor_scalar(reach[0:RP, :], base_f[0:RP, :], float(WIN), float(NB * P), ALU.add, ALU.min))
            step(ve.tensor_tensor(reach[0:RP, :], reach[0:RP, :], bound[0:RP, :], ALU.subtract))
            step(ve.tensor_scalar(reach[0:RP, :], reach[0:RP, :], float(P * (NB - ITERS + LAG)), None, ALU.is_gt))
            step(ve.tensor_reduce(bad[0:RP, 0:1], reach[0:RP, :], X, ALU.max))
            step(ve.tensor_tensor(bad[0:RP, 1:2], bad[0:RP, 1:2], bad[0:RP, 0:1], ALU.add))
            assert v.n == V_BAD
            dve.wait_ge(bad_sum, 1)
            step(ve.tensor_scalar(fast[0:RP, :], p_bad, 0.5, None, ALU.is_lt))
            ve.tensor_copy(fast_i[0:RP, :], fast[0:RP, :]).then_inc(flag_set, 1)
            step(ve.tensor_scalar(base_f[0:RP, :], base_f[0:RP, :], fast[0:RP, 0:1], None, ALU.mult))
            ve.tensor_copy(base_i[0:RP, :], base_f[0:RP, :]).then_inc(flag_set, 1)
            relative()
            assert v.n == V_LOC
            dve.wait_ge(flag_set, 2)
            flag = ve.value_load(fast_i[0:1, 0:1], min_val=0, max_val=1)

            def rsqrt(step, y, x, t):
                step(ve.tensor_scalar(t.bitcast(I32), x.bitcast(I32), 1, None, ALU.logical_shift_right))
                step(ve.tensor_scalar(y.bitcast(I32), t.bitcast(I32), -1.0, float(0x5F3759DF), ALU.mult, ALU.add))
                for _ in range(3):
                    step(ve.tensor_tensor(t, y, y, ALU.mult))
                    step(ve.scalar_tensor_tensor(t, t, -0.5, x, ALU.mult, ALU.mult))
                    step(ve.scalar_tensor_tensor(y, t, 1.5, y, ALU.add, ALU.mult))

            def inverse_root(scale, n):
                step(ve.tensor_scalar(deg[:, :], p_deg[n], 1.0, None, ALU.max))
                rsqrt(step, scale[:, :], deg[:, :], dtmp[:, :])

            def unturn(tables, n):
                for rb in range(RB):
                    k = n * RB + rb
                    dve.wait_ge(turned, k + 1)
                    for a, table in enumerate(tables):
                        ins = ve.tensor_scalar(table.rearrange("p (g h) -> p g h", h=TPG)[:, rb * RP:(rb + 1) * RP, :],
                                               p_rows[k % 2][:, a, :, 0:RP].rearrange("p h n -> p n h"),
                                               float(LOC_MAX) if a else 2 * FAR, None, ALU.min)
                    ins.then_inc(unturned, 1)
                dve.wait_ge(unturned, (n + 1) * RB)

            def split_ids():
                lo_i = loT.bitcast(I32)
                step(ve.tensor_copy(lo_i, hiT))
                step(ve.tensor_scalar(lo_i, lo_i, P - 1, None, ALU.bitwise_and))
                step(ve.tensor_copy(loT, lo_i))
                step(ve.tensor_tensor(hiT, hiT, loT, ALU.subtract))

            unturn((hiT, locT[:, TPI:]), 0)
            step(ve.tensor_scalar(idxT[:, TPI:], hiT, float(N - 1), None, ALU.min))
            assert v.n == V_IDX
            split_ids()
            assert v.n == V_IDS

            def degree_batch(before, buf, t0):
                dve.wait_ge(deg_mm, before + 1)
                ve.tensor_tensor(hlo[:, buf, :, :], iota[:, :].unsqueeze(1).to_broadcast([P, TPB, P]),
                                 loT[:, bass.ds(t0, TPB)].unsqueeze(2).to_broadcast([P, TPB, P]), ALU.is_equal)
                ve.tensor_tensor(hhi[:, buf, :, :], iota_hi[:, :].unsqueeze(1).to_broadcast([P, TPB, NB]),
                                 hiT[:, bass.ds(t0, TPB)].unsqueeze(2).to_broadcast([P, TPB, NB]), ALU.is_equal).then_inc(deg_oh, 1)

            with dve.Fori(0, SOLO) as it:
                for k in range(BPI):
                    degree_batch(it * BPI + k, k % 2, it * TPI + k * TPB)
            dve.wait_ge(x_sums, 2 * NB + 1)
            step(ve.tensor_scalar(mdif[:, :], mdif[:, :], 1.0 / D, 1e-5, ALU.mult, ALU.add))
            rsqrt(step, rstd[:, :], mdif[:, :], dtmp[:, :])
            with dve.Fori(0, PAIRS) as i:
                for k in range(2 * DBI):
                    degree_batch(i * (2 * DBI) + (SOLO * BPI + k), k % 2,
                                 i * (2 * TPI) + ((SOLO + k // DBI) * TPI + k % DBI * TPB))
            dve.wait_ge(deg_end, 1)
            inverse_root(out_s, 0)
            step(ve.tensor_tensor(rstd[:, :], rstd[:, :], out_s[:, :], ALU.mult))
            step(ve.tensor_tensor(mdif[:, :], mean[:, :], rstd[:, :], ALU.mult))
            dve.sem_inc(norm_set, 1)
            with dve.Fori(0, NXC) as c:
                for i in range(XC - XA):
                    b = c * XC + i
                    xb = xbig[:, bass.ds(b, 1), :].rearrange("p a d -> p (a d)")
                    ve.tensor_scalar(xb, xb, mean[:, bass.ds(b, 1)], rstd[:, bass.ds(b, 1)],
                                     ALU.add, ALU.mult).then_inc(normed, 1)
            unturn((hiT,), 1)
            split_ids()
            dve.wait_ge(table_out, 16 * (NXC + 1))
            ve.memset(aggT[:, 0:KD - 1, :], 0.0).then_inc(agg_zero, 1)
            dve.wait_ge(agg_zero, 2)
            dve.wait_ge(bases_in, 16)

            def add_group(where, psum, done):
                ve.tensor_tensor(aggT[:, :, where], aggT[:, :, where], psum, ALU.add).then_inc(done, 1)

            def one_hot(oh, local, tiles):
                return ve.tensor_tensor(oh, iota[:, 0:WIN].unsqueeze(1).to_broadcast([P, tiles, WIN]),
                                        local.unsqueeze(2).to_broadcast([P, tiles, WIN]), ALU.is_equal)

            def aggregate_batch(layer, it, k):
                col = (ITERS - it) * TPI if isinstance(it, int) else dve.snap(it * (-TPI) + ITERS * TPI, min_val=0)
                dve.wait_ge(agg_mm, it * GPI + (layer * ITERS * GPI + (k + 1) * (TPB // TPG)))
                one_hot(oneh[layer][:, k, :, :], locT[:, bass.ds(col + k * TPB, TPB)], TPB).then_inc(oh_set, 1)

            bases, loads = {}, []

            def load_bases(it, j):
                at = (ITERS - 1 - it) * GPI if isinstance(it, int) else dve.snap(it * (-GPI) + (ITERS - 1) * GPI, min_val=0)
                regs = [ve.alloc_register(f"base{j + k}_{len(loads)}") for k in range(BASES)]
                loads.append(j)
                ve.load(regs, base_l[0:1, bass.ds(at + j, BASES)])
                for k, reg in enumerate(regs):
                    bases[j + k] = dve.snap(reg, donate=True, min_val=0, max_val=N - 1)

            def aggregate_add(layer, it, j):
                done = it * GPI + (layer * ITERS * GPI + j)
                dve.wait_ge(agg_mm, done + (GPI + 1))
                dve.wait_ge(agg_add, done + AGG_SLOTS)
                add_group(bass.ds(bases[j], WIN), p_agg[j % AGG_SLOTS], agg_add)

            def aggregate_general(layer):
                with dve.Fori(0, NG) as g:
                    n0 = g * NW + layer * NG * NW
                    dve.wait_ge(gen_add, n0 + 1)
                    dve.wait_ge(gen_loc, g * (NW + 1) + (layer * NG * (NW + 1) + 1))
                    ve.tensor_copy(locw[:, :], locT[:, bass.ds(g * TPG + TPI, TPG)]).then_inc(gen_loc, 1)
                    with dve.Fori(0, NW) as w:
                        dve.wait_ge(gen_loc, g * (NW + 1) + w + (layer * NG * (NW + 1) + 2))
                        one_hot(oneh[layer][:, 0, 0:TPG, :], locw[:, :], TPG).then_inc(gen_oh, 1)
                        dve.wait_ge(gen_oh, n0 + w + 1)
                        ve.tensor_scalar(locw[:, :], locw[:, :], float(-WIN), None, ALU.add).then_inc(gen_loc, 1)
                        dve.wait_ge(gen_mm, n0 + w + 2)
                        add_group(bass.ds(w * WIN, WIN), p_agg[0], gen_add)
                        dve.wait_ge(gen_add, n0 + w + 2)
                        alone(dve, "dve")
                dve.sem_inc(agg_done, 1)

            with dve.If(flag):
                def batch(it, k):
                    aggregate_batch(0, it, k)
                    degree_batch(it * BPI + (DEG_ALL + k), k % 2, it * TPI + k * TPB)

                def iteration(it, last):
                    load_bases(it, 0)
                    for k in range(BPI):
                        if k + 1 < BPI:
                            batch(it, k + 1)
                        elif not last:
                            batch(it + 1, 0)
                        if k * (TPB // TPG) == BASES:
                            load_bases(it, BASES)
                        for j in range(k * (TPB // TPG), (k + 1) * (TPB // TPG)):
                            aggregate_add(0, it, j)

                batch(0, 0)
                with dve.Fori(0, ITERS - 1) as it:
                    iteration(it, False)
                iteration(ITERS - 1, True)
                dve.wait_ge(agg_add, ITERS * GPI + AGG_SLOTS)
                dve.sem_inc(agg_done, 1)
            with dve.Else():
                with dve.Fori(0, ITERS) as it:
                    for k in range(BPI):
                        degree_batch(it * BPI + (DEG_ALL + k), k % 2, it * TPI + k * TPB)
                aggregate_general(0)
            dve.wait_ge(deg_end, 2)
            inverse_root(in_s, 1)
            dve.wait_ge(consts_in, 16 * N_CONST)

            def conv_out(layer, psum, b, u, uses):
                dve.wait_ge(conv_mm[u], uses + 2)
                ve.scalar_tensor_tensor(tb[:, u, :], psum, in_s[:, bass.ds(b, 1)], cb[:, layer, :],
                                        ALU.mult, ALU.add).then_inc(conv_ev[u], 1)

            def conv_steps(i, first, last):
                left = ahead(dve, i, NXC // 2)

                def parts(n):
                    u, r, at = n % 2, n % XC, (-1 - n) % (2 * XC)
                    if n >= XC or not first:
                        dve.wait_ge(hb_set, i * (2 * XC) + (n - XC + 1))
                    dve.wait_ge(t_set, i * (2 * XC) + (n + 1))
                    ve.tensor_tensor(t_rest[:, r, :], t_exact[:, u, :], hb[:, at, 0, :], ALU.subtract).then_inc(rest_set, 1)
                    dve.wait_ge(rest_set, i * (2 * XC) + (n + 1))
                    ve.tensor_copy(hb[:, at, 1, :], t_rest[:, r, :]).then_inc(mid_set, 1)

                for n in range(2 * XC):
                    u, at = n % 2, 2 * XC - 1 - n
                    conv_out(0, p_conv1[u], left * (2 * XC) + at, u, i * XC + n // 2)
                    if n or not first:
                        parts(n - 1)
                if last:
                    parts(2 * XC - 1)

            conv_steps(0, True, False)
            with dve.Fori(1, NXC // 2 - 1) as i:
                conv_steps(i, False, False)
            conv_steps(NXC // 2 - 1, False, True)
            dve.wait_ge(cleared, NXC // 2)
            s = None

            def bs(ins):
                s.inc(ins)
                dve.wait_ge(bstep, s.now())

            def body(q, u, front, experts, it=None):
                m = 2 * q + u

                def add(j):
                    if it is not None:
                        aggregate_add(1, it, j)

                def batch(k):
                    if it is not None:
                        aggregate_batch(1, it + k // BPI, k % BPI)

                if it is not None:
                    load_bases(it, 0)
                add(0)
                w = 1 - u
                if front:
                    conv_out(1, p_conv, ahead(dve, q, HB) * 2 + (1 - u), u, q + HB)
                    dve.wait_ge(conv_ev[u], q + (HB + 2))
                    dve.wait_ge(xin_in[u], q * 16 + 16)
                    ve.scalar_tensor_tensor(xr[:, u, :], tb[:, u, :], 0.0, xin[:, u, :], ALU.max, ALU.add).then_inc(xr_set, 1)
                add(1)
                if front:
                    dve.wait_ge(xr_set, m + 1)
                    bs(ve.bn_stats(st6[:, :], xr[:, u, :]))
                    alone(dve, "dve")
                    bs(ve.bn_aggr(mv[:, :], st6[:, :]))
                    bs(ve.tensor_scalar(rv[:, :], mv[:, 1:2], 1e-5, None, ALU.add))
                    rsqrt(bs, rs[:, :], rv[:, :], rt[:, :])
                    need(dve, xnT_mm, m)
                    ve.tensor_scalar(xn[:, :], xr[:, u, :], mv[:, 0:1], rs[:, 0:1], ALU.subtract, ALU.mult).then_inc(xn_set, 1)
                    dve.wait_ge(xn_set, m + 1)
                if experts:
                    dve.wait_ge(acc_free[w], q + u)
                    dve.wait_ge(b3_mm, m + 1)
                    ve.tensor_tensor(acc[:, w, :], xr[:, w, :], p_b3, ALU.add).then_inc(acc_init, 1)
                    dve.wait_ge(acc_init, m + 1)
                    dve.wait_ge(gate_set, m)

                def add_expert(e):
                    k = (m - 1) * NE + e
                    dve.wait_ge(h3_mm, k + 3)
                    if e:
                        dve.wait_ge(h3_ev, k + 3)
                    ve.scalar_tensor_tensor(acc[:, w, :], exp_bank("l3", e, w), gate[:, w, e:e + 1], acc[:, w, :],
                                            ALU.mult, ALU.add).then_inc(h3_ev, 1)

                batch(2)
                for e in range(NE - 2):
                    if it is not None and e + 2 == BASES:
                        load_bases(it, BASES)
                    add(e + 2)
                    if e == 1:
                        batch(3)
                    if experts:
                        add_expert(e)
                    if e > 1:
                        batch(BPI + e - 2)
                if front:
                    dve.wait_ge(lg_mm, m + 1)
                    bs(ve.tensor_tensor(lg[:, :], p_lg, rb2[:, :], ALU.add))
                    ve.tensor_reduce(lmax[:, :], lg[:, :], X, ALU.max, negate=True).then_inc(lmax_set, 1)
                add(NE)
                if experts:
                    add_expert(NE - 2)
                if front:
                    dve.wait_ge(pe_set, m + 1)
                    bs(ve.reciprocal(psumr[:, :], psumr[:, :]))
                    bs(ve.tensor_scalar(prob[:, 0:NE], pexp[:, :], psumr[:, 0:1], None, ALU.mult))
                    alone(dve, "dve")
                    bs(ve.max(top[:, :], prob[:, :]))
                    ve.tensor_tensor(w12[:, 0:1], top[:, 1:2], top[:, 0:1], ALU.subtract).then_inc(wd_set, 1)
                    bs(ve.max_index(topi[:, :], top[:, :], prob[:, :]))
                    bs(ve.tensor_copy(topf[:, :], topi[:, :]))
                add(NE + 1)
                if experts:
                    add_expert(NE - 1)
                if front:
                    dve.wait_ge(wx_set, m + 1)
                    bs(ve.tensor_scalar(w12[:, 2:3], w12[:, 1:2], 1.0, None, ALU.add))
                    bs(ve.reciprocal(w12[:, 3:4], w12[:, 2:3]))
                    bs(ve.tensor_tensor(w12[:, 2:3], w12[:, 1:2], w12[:, 3:4], ALU.mult))
                    bs(ve.tensor_scalar(gt2[:, :], iota[:, 0:NE], topf[:, 1:2], w12[:, 2:3], ALU.is_equal, ALU.mult))
                    bs(ve.tensor_scalar(gate[:, u, :], iota[:, 0:NE], topf[:, 0:1], w12[:, 3:4], ALU.is_equal, ALU.mult))
                    ve.tensor_tensor(gate[:, u, :], gate[:, u, :], gt2[:, :], ALU.add).then_inc(gate_set, 1)

            PER_FRONT = 3 + 11 + 1 + 5 + 5

            def counted(q, u, front, experts, it=None):
                if not isinstance(q, int) and u == 1:
                    s.enter(q, 2 * PER_FRONT)
                body(q, u, front, experts, it)
                if not isinstance(q, int) and u == 0:
                    s.leave(HB - 1)

            with dve.If(flag):
                aggregate_batch(1, 0, 0)
                aggregate_batch(1, 0, 1)
                s = Steps(bstep)
                fused(dve, counted)
            with dve.Else():
                aggregate_general(1)
                s = Steps(bstep)
                bodies(dve, counted)


_INS = ["x", "src", "dst", "L0_gnn_W1", "L0_gnn_b1", "L0_gnn_W2", "L0_gnn_b2", "L0_ffn_router_w1", "L0_ffn_router_b1",
        "L0_ffn_router_w2", "L0_ffn_router_b2", "L0_ffn_expert_w1", "L0_ffn_expert_b1", "L0_ffn_expert_w2",
        "L0_ffn_expert_b2", "L0_ffn_expert_w3", "L0_ffn_expert_b3"]


def kernel(**inputs):
    import numpy as _np
    import concourse.bacc as _bacc
    from concourse import mybir as _mybir
    from concourse.bass_utils import run_bass_kernel_spmd as _run

    nc = _bacc.Bacc("TRN2", target_bir_lowering=False, num_devices=1)
    arrays, args = {}, {}
    for name in _INS:
        a = _np.ascontiguousarray(inputs[name])
        arrays[f"in_{name}_dram"] = a
        args[name] = nc.dram_tensor(f"in_{name}_dram", a.shape, _mybir.dt.from_np(a.dtype), kind="ExternalInput").ap()
    out = nc.dram_tensor("out_dram", arrays["in_x_dram"].shape, _mybir.dt.float32, kind="ExternalOutput").ap()
    gnn_experts(nc, args, out)
    r = _run(nc, [arrays], core_ids=[0])
    return r.results[0]["out_dram"]
```
